# Optimizing a Trainium2 kernel written in Bass

```python
import numpy as np
import jax
import jax.numpy as jnp

def _softmax(x, axis=-1):
    return jax.nn.softmax(x, axis=axis)

def _gelu(x):
    return jax.nn.gelu(x, approximate=True)

def _silu(x):
    return jax.nn.silu(x)

def _sigmoid(x):
    return jax.nn.sigmoid(x)

def _layernorm(x, axis=-1, eps=1e-05):
    m = jnp.mean(x, axis=axis, keepdims=True)
    v = jnp.var(x, axis=axis, keepdims=True)
    return (x - m) / jnp.sqrt(v + eps)

def _scatter_add(tgt, idx, src, axis=0):
    return tgt.at[idx].add(src)

def _segment_sum(src, seg, n):
    return jax.ops.segment_sum(src, seg, n)
kernel_name = 'mk_xattn_seq_d4_seqx_r8_95a095'

def setup_inputs(seed: int=0):
    np.random.seed(seed)
    _w = jnp.asarray

    def _rec_inputs():
        import jax
        import jax.numpy as jnp
        _rk = jax.random.key(seed)
        x = 7.22e-05 + 1 * jax.random.normal(jax.random.fold_in(_rk, 1), (8, 128, 256), jnp.float32)
        _lenS = 128 - jax.random.randint(jax.random.fold_in(_rk, 7), (8,), 0, max(1, 128 // 4) + 1, jnp.int32)
        _lenS2 = 128 - jax.random.randint(jax.random.fold_in(_rk, 8), (8,), 0, max(1, 128 // 4) + 1, jnp.int32)
        _ctx_2048P = jax.random.normal(jax.random.fold_in(_rk, 11), (8, 16, 256), jnp.float32)
        _ctx_2048c = jax.random.dirichlet(jax.random.fold_in(_rk, 511), 0.3 * jnp.ones((16,), jnp.float32), (8, 128))
        _ctx_2048t = jnp.einsum('bsk,bkd->bsd', _ctx_2048c, _ctx_2048P)
        _ctx_2048t = _ctx_2048t * jax.lax.rsqrt(jnp.mean(jnp.square(_ctx_2048t)) + 1e-12) * 0.953939
        ctx_2048 = 2.81802e-05 + 1.00001 * (_ctx_2048t + 0.3 * jax.random.normal(jax.random.fold_in(_rk, 611), (8, 128, 256), jnp.float32))
        _validS = jnp.arange(128)[None, :] < _lenS[:, None]
        _validS2 = jnp.arange(128)[None, :] < _lenS2[:, None]
        _causal = jnp.tril(jnp.ones((128, 128), dtype=bool))
        mask_BxS2_bf1 = jnp.ones((8, 128), dtype=bool)
        mask_BxS2_ik0 = jnp.where(jnp.broadcast_to(_validS2[:, :], (8, 128)), 0, 1).astype(jnp.int32)
        mask_1x1xSxS2_fc1 = jnp.where(jnp.broadcast_to(_validS2[0:1, None, None, :], (1, 1, 128, 128)), 1.0, 0.0).astype(jnp.float32)
        mask_Bx1xSxS2_ff1 = jnp.where(jnp.ones((8, 1, 128, 128), dtype=bool), 1.0, 0.0).astype(jnp.float32)
        return (x, ctx_2048, mask_BxS2_bf1, mask_BxS2_ik0, mask_1x1xSxS2_fc1, mask_Bx1xSxS2_ff1)
    x, ctx_2048, mask_BxS2_bf1, mask_BxS2_ik0, mask_1x1xSxS2_fc1, mask_Bx1xSxS2_ff1 = _rec_inputs()

    def _L0_xattn_setup():
        import jax, jax.numpy as jnp
        import numpy as np
        D = 256
        H = 16
        HD = D // H
        INNER = 4 * D
        EPS = 1e-05

        def layer_norm(x, w, b):
            mu = jnp.mean(x, axis=-1, keepdims=True)
            var = jnp.mean(jnp.square(x - mu), axis=-1, keepdims=True)
            return (x - mu) * jax.lax.rsqrt(var + EPS) * w + b
        key = jax.random.key(seed)
        ks = jax.random.split(key, 12)
        B, LQ, LK = (4, 128, 256)
        std = 0.02
        inp = {'hidden_states': jax.random.normal(ks[0], (B, LQ, D), jnp.float32), 'encoder_hidden_states': jax.random.normal(ks[1], (B, LK, D), jnp.float32), 'encoder_attention_mask': jnp.ones((B, LK), dtype=bool), 'ln1_w': jnp.ones((D,), jnp.float32), 'ln1_b': jnp.zeros((D,), jnp.float32), 'q_w': jax.random.normal(ks[2], (D, D), jnp.float32) * std, 'q_b': jnp.zeros((D,), jnp.float32), 'k_w': jax.random.normal(ks[3], (D, D), jnp.float32) * std, 'k_b': jnp.zeros((D,), jnp.float32), 'v_w': jax.random.normal(ks[4], (D, D), jnp.float32) * std, 'v_b': jnp.zeros((D,), jnp.float32), 'cproj_w': jax.random.normal(ks[5], (D, D), jnp.float32) * std, 'cproj_b': jnp.zeros((D,), jnp.float32), 'ln2_w': jnp.ones((D,), jnp.float32), 'ln2_b': jnp.zeros((D,), jnp.float32), 'fc_w': jax.random.normal(ks[6], (D, INNER), jnp.float32) * std, 'fc_b': jnp.zeros((INNER,), jnp.float32), 'proj_w': jax.random.normal(ks[7], (INNER, D), jnp.float32) * std, 'proj_b': jnp.zeros((D,), jnp.float32)}
        return inp
    _L0_xattn_all = _L0_xattn_setup()
    _L0_xattn_in = {k: v for k, v in _L0_xattn_all.items() if k in ('ln1_w', 'ln1_b', 'q_w', 'q_b', 'k_w', 'k_b', 'v_w', 'v_b', 'cproj_w', 'cproj_b', 'ln2_w', 'ln2_b', 'fc_w', 'fc_b', 'proj_w', 'proj_b')}
    del _L0_xattn_all

    def _L1_xattn_setup():
        import jax, jax.numpy as jnp
        import numpy as np
        B, P, K, H, NH = (4, 256, 32, 256, 16)
        DH = H // NH
        EPS = 1e-06

        def rmsnorm(x, w):
            var = jnp.mean(jnp.square(x), axis=-1, keepdims=True)
            return x * jax.lax.rsqrt(var + EPS) * w
        key = jax.random.key(seed)
        ks = jax.random.split(key, 12)
        s = 0.02
        return {'x': jax.random.normal(ks[0], (B, P, H), jnp.float32), 'latents': jax.random.normal(ks[1], (B, K, H), jnp.float32), 'attention_mask': jax.random.randint(ks[2], (B, P), 0, 2, jnp.int32), 'q_w': s * jax.random.normal(ks[3], (H, H), jnp.float32), 'q_b': jnp.zeros((H,), jnp.float32), 'kv_w': s * jax.random.normal(ks[4], (H, 2 * H), jnp.float32), 'kv_b': jnp.zeros((2 * H,), jnp.float32), 'out_w': s * jax.random.normal(ks[5], (H, H), jnp.float32), 'out_b': jnp.zeros((H,), jnp.float32), 'postnorm_w': jnp.ones((H,), jnp.float32), 'mlp_w1': s * jax.random.normal(ks[6], (H, 4 * H), jnp.float32), 'mlp_b1': jnp.zeros((4 * H,), jnp.float32), 'mlp_w2': s * jax.random.normal(ks[7], (4 * H, H), jnp.float32), 'mlp_b2': jnp.zeros((H,), jnp.float32)}
    _L1_xattn_all = _L1_xattn_setup()
    _L1_xattn_in = {k: v for k, v in _L1_xattn_all.items() if k in ('q_w', 'q_b', 'kv_w', 'kv_b', 'out_w', 'out_b', 'postnorm_w', 'mlp_w1', 'mlp_b1', 'mlp_w2', 'mlp_b2')}
    del _L1_xattn_all

    def _L2_xattn_setup():
        import jax, jax.numpy as jnp
        import numpy as np
        B, Q, S1, S2 = (4, 32, 256, 256)
        D, H, K, F = (256, 16, 128, 1024)
        LN_EPS = 1e-05

        def _layer_norm(x, scale, offset):
            mu = jnp.mean(x, axis=-1, keepdims=True)
            var = jnp.var(x, axis=-1, keepdims=True)
            return (x - mu) * jax.lax.rsqrt(var + LN_EPS) * scale + offset

        def _cross_attention(q_in, kv_in, wq, bq, wk, bk, wv, bv, wo, bo, bias_k, bias_v):
            b, q_len, _ = q_in.shape
            t = kv_in.shape[1]
            qh = (q_in @ wq + bq).reshape(b, q_len, H, K)
            kh = (kv_in @ wk + bk).reshape(b, t, H, K)
            vh = (kv_in @ wv + bv).reshape(b, t, H, K)
            kh = jnp.concatenate([kh, jnp.broadcast_to(bias_k, (b, 1, H, K))], axis=1)
            vh = jnp.concatenate([vh, jnp.broadcast_to(bias_v, (b, 1, H, K))], axis=1)
            scale = jnp.sqrt(jnp.asarray(K, q_in.dtype))
            logits = jnp.einsum('bqhk,bthk->bhqt', qh, kh) / scale
            weights = jax.nn.softmax(logits, axis=-1)
            ctx = jnp.einsum('bhqt,bthk->bqhk', weights, vh).reshape(b, q_len, H * K)
            return ctx @ wo + bo

        def _forward(x, xf_1, xf_2, ln1_scale, ln1_offset, wq1, bq1, wk1, bk1, wv1, bv1, wo1, bo1, bias_k1, bias_v1, ln2_scale, ln2_offset, wq2, bq2, wk2, bk2, wv2, bv2, wo2, bo2, bias_k2, bias_v2, ln_mlp_scale, ln_mlp_offset, w_fc1, b_fc1, w_fc2, b_fc2):
            res = x
            h = _layer_norm(x, ln1_scale, ln1_offset)
            x = res + _cross_attention(h, xf_1, wq1, bq1, wk1, bk1, wv1, bv1, wo1, bo1, bias_k1, bias_v1)
            res = x
            h = _layer_norm(x, ln2_scale, ln2_offset)
            x = res + _cross_attention(h, xf_2, wq2, bq2, wk2, bk2, wv2, bv2, wo2, bo2, bias_k2, bias_v2)
            h = _layer_norm(x, ln_mlp_scale, ln_mlp_offset)
            h = jax.nn.gelu(h @ w_fc1 + b_fc1, approximate=False) @ w_fc2 + b_fc2
            return x + h
        key = jax.random.key(seed)
        ks = iter(jax.random.split(key, 64))

        def rn(shape, s=0.02):
            return jax.random.normal(next(ks), shape, jnp.float32) * s
        inp = {'x': rn((B, Q, D), 1.0), 'xf_1': rn((B, S1, D), 1.0), 'xf_2': rn((B, S2, D), 1.0)}
        for i in (1, 2):
            inp[f'ln{i}_scale'] = jnp.ones((D,), jnp.float32)
            inp[f'ln{i}_offset'] = jnp.zeros((D,), jnp.float32)
            inp[f'wq{i}'] = rn((D, H * K))
            inp[f'bq{i}'] = jnp.zeros((H * K,), jnp.float32)
            inp[f'wk{i}'] = rn((D, H * K))
            inp[f'bk{i}'] = jnp.zeros((H * K,), jnp.float32)
            inp[f'wv{i}'] = rn((D, H * K))
            inp[f'bv{i}'] = jnp.zeros((H * K,), jnp.float32)
            inp[f'wo{i}'] = rn((H * K, D))
            inp[f'bo{i}'] = jnp.zeros((D,), jnp.float32)
            inp[f'bias_k{i}'] = rn((1, 1, H, K))
            inp[f'bias_v{i}'] = rn((1, 1, H, K))
        inp['ln_mlp_scale'] = jnp.ones((D,), jnp.float32)
        inp['ln_mlp_offset'] = jnp.zeros((D,), jnp.float32)
        inp['w_fc1'] = rn((D, F))
        inp['b_fc1'] = jnp.zeros((F,), jnp.float32)
        inp['w_fc2'] = rn((F, D))
        inp['b_fc2'] = jnp.zeros((D,), jnp.float32)
        return inp
    _L2_xattn_all = _L2_xattn_setup()
    _L2_xattn_in = {k: v for k, v in _L2_xattn_all.items() if k in ('ln1_scale', 'ln1_offset', 'wq1', 'bq1', 'wk1', 'bk1', 'wv1', 'bv1', 'wo1', 'bo1', 'bias_k1', 'bias_v1', 'ln2_scale', 'ln2_offset', 'wq2', 'bq2', 'wk2', 'bk2', 'wv2', 'bv2', 'wo2', 'bo2', 'bias_k2', 'bias_v2', 'ln_mlp_scale', 'ln_mlp_offset', 'w_fc1', 'b_fc1', 'w_fc2', 'b_fc2')}
    del _L2_xattn_all

    def _L3_xattn_setup():
        import jax, jax.numpy as jnp
        import numpy as np
        H = 256
        NH = 16
        HD = H // NH
        EPS = 1e-05

        def gelu(x):
            return 0.5 * x * (1.0 + jnp.tanh(0.7978845608028654 * x * (1.0 + 0.044715 * x * x)))

        def layernorm(x, scale, bias):
            m = jnp.mean(x, axis=-1, keepdims=True)
            v = jnp.mean(jnp.square(x - m), axis=-1, keepdims=True)
            return (x - m) * jax.lax.rsqrt(v + EPS) * scale + bias

        def split_heads(x):
            b, s, _ = x.shape
            return x.reshape(b, s, NH, HD).transpose(0, 2, 1, 3)

        def merge_heads(x):
            b, nh, s, hd = x.shape
            return x.transpose(0, 2, 1, 3).reshape(b, s, nh * hd)

        def attention(q, k, v, mask):
            scores = jnp.einsum('bhqd,bhkd->bhqk', q, k) / jnp.sqrt(jnp.float32(HD))
            scores = scores * mask - 10000.0 * (1.0 - mask)
            probs = jax.nn.softmax(scores, axis=-1)
            return jnp.einsum('bhqk,bhkd->bhqd', probs, v)
        key = jax.random.key(seed)
        ks = jax.random.split(key, 16)
        b, s, t = (2, 128, 128)
        w = lambda k, i, o: jax.random.normal(k, (i, o), jnp.float32) * 0.02
        inp = {'hidden_states': jax.random.normal(ks[0], (b, s, H), jnp.float32), 'encoder_states': jax.random.normal(ks[1], (b, t, H), jnp.float32), 'ltor_mask': jnp.tril(jnp.ones((1, 1, s, s), jnp.float32)), 'cross_mask': jnp.ones((b, 1, s, t), jnp.float32), 'ln1_s': jnp.ones((H,), jnp.float32), 'ln1_b': jnp.zeros((H,), jnp.float32), 'w_qkv': w(ks[2], H, 3 * H), 'b_qkv': jnp.zeros((3 * H,), jnp.float32), 'w_ao': w(ks[3], H, H), 'b_ao': jnp.zeros((H,), jnp.float32), 'ln2_s': jnp.ones((H,), jnp.float32), 'ln2_b': jnp.zeros((H,), jnp.float32), 'w_q': w(ks[4], H, H), 'b_q': jnp.zeros((H,), jnp.float32), 'w_kv': w(ks[5], H, 2 * H), 'b_kv': jnp.zeros((2 * H,), jnp.float32), 'w_co': w(ks[6], H, H), 'b_co': jnp.zeros((H,), jnp.float32), 'ln3_s': jnp.ones((H,), jnp.float32), 'ln3_b': jnp.zeros((H,), jnp.float32), 'w1': w(ks[7], H, 4 * H), 'b1': jnp.zeros((4 * H,), jnp.float32), 'w2': w(ks[8], 4 * H, H), 'b2': jnp.zeros((H,), jnp.float32)}
        return inp
    _L3_xattn_all = _L3_xattn_setup()
    _L3_xattn_in = {k: v for k, v in _L3_xattn_all.items() if k in ('ln1_s', 'ln1_b', 'w_qkv', 'b_qkv', 'w_ao', 'b_ao', 'ln2_s', 'ln2_b', 'w_q', 'b_q', 'w_kv', 'b_kv', 'w_co', 'b_co', 'ln3_s', 'ln3_b', 'w1', 'b1', 'w2', 'b2')}
    del _L3_xattn_all
    return {'x': x, 'ctx_2048': ctx_2048, 'mask_BxS2_bf1': mask_BxS2_bf1, 'mask_BxS2_ik0': mask_BxS2_ik0, 'mask_1x1xSxS2_fc1': mask_1x1xSxS2_fc1, 'mask_Bx1xSxS2_ff1': mask_Bx1xSxS2_ff1, 'L0_xattn_ln1_w': _L0_xattn_in['ln1_w'], 'L0_xattn_ln1_b': _L0_xattn_in['ln1_b'], 'L0_xattn_q_w': _L0_xattn_in['q_w'], 'L0_xattn_q_b': _L0_xattn_in['q_b'], 'L0_xattn_k_w': _L0_xattn_in['k_w'], 'L0_xattn_k_b': _L0_xattn_in['k_b'], 'L0_xattn_v_w': _L0_xattn_in['v_w'], 'L0_xattn_v_b': _L0_xattn_in['v_b'], 'L0_xattn_cproj_w': _L0_xattn_in['cproj_w'], 'L0_xattn_cproj_b': _L0_xattn_in['cproj_b'], 'L0_xattn_ln2_w': _L0_xattn_in['ln2_w'], 'L0_xattn_ln2_b': _L0_xattn_in['ln2_b'], 'L0_xattn_fc_w': _L0_xattn_in['fc_w'], 'L0_xattn_fc_b': _L0_xattn_in['fc_b'], 'L0_xattn_proj_w': _L0_xattn_in['proj_w'], 'L0_xattn_proj_b': _L0_xattn_in['proj_b'], 'L1_xattn_q_w': _L1_xattn_in['q_w'], 'L1_xattn_q_b': _L1_xattn_in['q_b'], 'L1_xattn_kv_w': _L1_xattn_in['kv_w'], 'L1_xattn_kv_b': _L1_xattn_in['kv_b'], 'L1_xattn_out_w': _L1_xattn_in['out_w'], 'L1_xattn_out_b': _L1_xattn_in['out_b'], 'L1_xattn_postnorm_w': _L1_xattn_in['postnorm_w'], 'L1_xattn_mlp_w1': _L1_xattn_in['mlp_w1'], 'L1_xattn_mlp_b1': _L1_xattn_in['mlp_b1'], 'L1_xattn_mlp_w2': _L1_xattn_in['mlp_w2'], 'L1_xattn_mlp_b2': _L1_xattn_in['mlp_b2'], 'L2_xattn_ln1_scale': _L2_xattn_in['ln1_scale'], 'L2_xattn_ln1_offset': _L2_xattn_in['ln1_offset'], 'L2_xattn_wq1': _L2_xattn_in['wq1'], 'L2_xattn_bq1': _L2_xattn_in['bq1'], 'L2_xattn_wk1': _L2_xattn_in['wk1'], 'L2_xattn_bk1': _L2_xattn_in['bk1'], 'L2_xattn_wv1': _L2_xattn_in['wv1'], 'L2_xattn_bv1': _L2_xattn_in['bv1'], 'L2_xattn_wo1': _L2_xattn_in['wo1'], 'L2_xattn_bo1': _L2_xattn_in['bo1'], 'L2_xattn_bias_k1': _L2_xattn_in['bias_k1'], 'L2_xattn_bias_v1': _L2_xattn_in['bias_v1'], 'L2_xattn_ln2_scale': _L2_xattn_in['ln2_scale'], 'L2_xattn_ln2_offset': _L2_xattn_in['ln2_offset'], 'L2_xattn_wq2': _L2_xattn_in['wq2'], 'L2_xattn_bq2': _L2_xattn_in['bq2'], 'L2_xattn_wk2': _L2_xattn_in['wk2'], 'L2_xattn_bk2': _L2_xattn_in['bk2'], 'L2_xattn_wv2': _L2_xattn_in['wv2'], 'L2_xattn_bv2': _L2_xattn_in['bv2'], 'L2_xattn_wo2': _L2_xattn_in['wo2'], 'L2_xattn_bo2': _L2_xattn_in['bo2'], 'L2_xattn_bias_k2': _L2_xattn_in['bias_k2'], 'L2_xattn_bias_v2': _L2_xattn_in['bias_v2'], 'L2_xattn_ln_mlp_scale': _L2_xattn_in['ln_mlp_scale'], 'L2_xattn_ln_mlp_offset': _L2_xattn_in['ln_mlp_offset'], 'L2_xattn_w_fc1': _L2_xattn_in['w_fc1'], 'L2_xattn_b_fc1': _L2_xattn_in['b_fc1'], 'L2_xattn_w_fc2': _L2_xattn_in['w_fc2'], 'L2_xattn_b_fc2': _L2_xattn_in['b_fc2'], 'L3_xattn_ln1_s': _L3_xattn_in['ln1_s'], 'L3_xattn_ln1_b': _L3_xattn_in['ln1_b'], 'L3_xattn_w_qkv': _L3_xattn_in['w_qkv'], 'L3_xattn_b_qkv': _L3_xattn_in['b_qkv'], 'L3_xattn_w_ao': _L3_xattn_in['w_ao'], 'L3_xattn_b_ao': _L3_xattn_in['b_ao'], 'L3_xattn_ln2_s': _L3_xattn_in['ln2_s'], 'L3_xattn_ln2_b': _L3_xattn_in['ln2_b'], 'L3_xattn_w_q': _L3_xattn_in['w_q'], 'L3_xattn_b_q': _L3_xattn_in['b_q'], 'L3_xattn_w_kv': _L3_xattn_in['w_kv'], 'L3_xattn_b_kv': _L3_xattn_in['b_kv'], 'L3_xattn_w_co': _L3_xattn_in['w_co'], 'L3_xattn_b_co': _L3_xattn_in['b_co'], 'L3_xattn_ln3_s': _L3_xattn_in['ln3_s'], 'L3_xattn_ln3_b': _L3_xattn_in['ln3_b'], 'L3_xattn_w1': _L3_xattn_in['w1'], 'L3_xattn_b1': _L3_xattn_in['b1'], 'L3_xattn_w2': _L3_xattn_in['w2'], 'L3_xattn_b2': _L3_xattn_in['b2']}

def reference(x, ctx_2048, mask_BxS2_bf1, mask_BxS2_ik0, mask_1x1xSxS2_fc1, mask_Bx1xSxS2_ff1, L0_xattn_ln1_w, L0_xattn_ln1_b, L0_xattn_q_w, L0_xattn_q_b, L0_xattn_k_w, L0_xattn_k_b, L0_xattn_v_w, L0_xattn_v_b, L0_xattn_cproj_w, L0_xattn_cproj_b, L0_xattn_ln2_w, L0_xattn_ln2_b, L0_xattn_fc_w, L0_xattn_fc_b, L0_xattn_proj_w, L0_xattn_proj_b, L1_xattn_q_w, L1_xattn_q_b, L1_xattn_kv_w, L1_xattn_kv_b, L1_xattn_out_w, L1_xattn_out_b, L1_xattn_postnorm_w, L1_xattn_mlp_w1, L1_xattn_mlp_b1, L1_xattn_mlp_w2, L1_xattn_mlp_b2, L2_xattn_ln1_scale, L2_xattn_ln1_offset, L2_xattn_wq1, L2_xattn_bq1, L2_xattn_wk1, L2_xattn_bk1, L2_xattn_wv1, L2_xattn_bv1, L2_xattn_wo1, L2_xattn_bo1, L2_xattn_bias_k1, L2_xattn_bias_v1, L2_xattn_ln2_scale, L2_xattn_ln2_offset, L2_xattn_wq2, L2_xattn_bq2, L2_xattn_wk2, L2_xattn_bk2, L2_xattn_wv2, L2_xattn_bv2, L2_xattn_wo2, L2_xattn_bo2, L2_xattn_bias_k2, L2_xattn_bias_v2, L2_xattn_ln_mlp_scale, L2_xattn_ln_mlp_offset, L2_xattn_w_fc1, L2_xattn_b_fc1, L2_xattn_w_fc2, L2_xattn_b_fc2, L3_xattn_ln1_s, L3_xattn_ln1_b, L3_xattn_w_qkv, L3_xattn_b_qkv, L3_xattn_w_ao, L3_xattn_b_ao, L3_xattn_ln2_s, L3_xattn_ln2_b, L3_xattn_w_q, L3_xattn_b_q, L3_xattn_w_kv, L3_xattn_b_kv, L3_xattn_w_co, L3_xattn_b_co, L3_xattn_ln3_s, L3_xattn_ln3_b, L3_xattn_w1, L3_xattn_b1, L3_xattn_w2, L3_xattn_b2):
    import jax
    import jax.numpy as jnp

    def _L0_xattn_ref(hidden_states, encoder_hidden_states, encoder_attention_mask, ln1_w, ln1_b, q_w, q_b, k_w, k_b, v_w, v_b, cproj_w, cproj_b, ln2_w, ln2_b, fc_w, fc_b, proj_w, proj_b):
        import jax, jax.numpy as jnp
        import numpy as np
        D = 256
        H = 16
        HD = D // H
        INNER = 4 * D
        EPS = 1e-05

        def layer_norm(x, w, b):
            mu = jnp.mean(x, axis=-1, keepdims=True)
            var = jnp.mean(jnp.square(x - mu), axis=-1, keepdims=True)
            return (x - mu) * jax.lax.rsqrt(var + EPS) * w + b
        B, LQ, _ = hidden_states.shape
        LK = encoder_hidden_states.shape[1]
        residual = hidden_states
        x = layer_norm(hidden_states, ln1_w, ln1_b)
        q = (x @ q_w + q_b).reshape(B, LQ, H, HD).transpose(0, 2, 1, 3)
        k = (encoder_hidden_states @ k_w + k_b).reshape(B, LK, H, HD).transpose(0, 2, 1, 3)
        v = (encoder_hidden_states @ v_w + v_b).reshape(B, LK, H, HD).transpose(0, 2, 1, 3)
        scale = 1.0 / np.sqrt(HD).astype(np.float32)
        scores = jnp.einsum('bhqd,bhkd->bhqk', q, k) * scale
        mask = encoder_attention_mask[:, None, None, :]
        mask_value = jnp.finfo(scores.dtype).min
        scores = jnp.where(mask, scores, mask_value)
        attn = jax.nn.softmax(scores, axis=-1)
        out = jnp.einsum('bhqk,bhkd->bhqd', attn, v)
        out = out.transpose(0, 2, 1, 3).reshape(B, LQ, D)
        out = out @ cproj_w + cproj_b
        hidden = out + residual
        residual = hidden
        y = layer_norm(hidden, ln2_w, ln2_b)
        y = jax.nn.gelu(y @ fc_w + fc_b, approximate=True)
        y = y @ proj_w + proj_b
        return residual + y

    def _L1_xattn_ref(x, latents, attention_mask, q_w, q_b, kv_w, kv_b, out_w, out_b, postnorm_w, mlp_w1, mlp_b1, mlp_w2, mlp_b2):
        import jax, jax.numpy as jnp
        import numpy as np
        B, P, K, H, NH = (4, 256, 32, 256, 16)
        DH = H // NH
        EPS = 1e-06

        def rmsnorm(x, w):
            var = jnp.mean(jnp.square(x), axis=-1, keepdims=True)
            return x * jax.lax.rsqrt(var + EPS) * w
        b, p, _ = x.shape
        k_len = latents.shape[1]
        residual = latents
        h = jnp.concatenate([x, latents], axis=1)
        q = (latents @ q_w + q_b).reshape(b, k_len, NH, DH)
        kv = (h @ kv_w + kv_b).reshape(b, p + k_len, NH, DH, 2)
        kmat, v = (kv[..., 0], kv[..., 1])
        attn = jnp.einsum('bkhd,bnhd->bhkn', q, kmat) / DH
        full_mask = jnp.concatenate([attention_mask.astype(bool), jnp.ones((b, k_len), bool)], axis=-1)
        attn = jnp.where(full_mask[:, None, None, :], attn, -jnp.inf)
        attn = jax.nn.softmax(attn.astype(jnp.float32), axis=-1).astype(q.dtype)
        attn_out = jnp.einsum('bhkn,bnhd->bkhd', attn, v).reshape(b, k_len, H)
        attn_out = attn_out @ out_w + out_b + residual
        out = rmsnorm(attn_out, postnorm_w)
        out = jax.nn.gelu(out @ mlp_w1 + mlp_b1) @ mlp_w2 + mlp_b2
        return out + residual

    def _L2_xattn_ref(x, xf_1, xf_2, ln1_scale, ln1_offset, wq1, bq1, wk1, bk1, wv1, bv1, wo1, bo1, bias_k1, bias_v1, ln2_scale, ln2_offset, wq2, bq2, wk2, bk2, wv2, bv2, wo2, bo2, bias_k2, bias_v2, ln_mlp_scale, ln_mlp_offset, w_fc1, b_fc1, w_fc2, b_fc2):
        import jax, jax.numpy as jnp
        import numpy as np
        B, Q, S1, S2 = (4, 32, 256, 256)
        D, H, K, F = (256, 16, 128, 1024)
        LN_EPS = 1e-05

        def _layer_norm(x, scale, offset):
            mu = jnp.mean(x, axis=-1, keepdims=True)
            var = jnp.var(x, axis=-1, keepdims=True)
            return (x - mu) * jax.lax.rsqrt(var + LN_EPS) * scale + offset

        def _cross_attention(q_in, kv_in, wq, bq, wk, bk, wv, bv, wo, bo, bias_k, bias_v):
            b, q_len, _ = q_in.shape
            t = kv_in.shape[1]
            qh = (q_in @ wq + bq).reshape(b, q_len, H, K)
            kh = (kv_in @ wk + bk).reshape(b, t, H, K)
            vh = (kv_in @ wv + bv).reshape(b, t, H, K)
            kh = jnp.concatenate([kh, jnp.broadcast_to(bias_k, (b, 1, H, K))], axis=1)
            vh = jnp.concatenate([vh, jnp.broadcast_to(bias_v, (b, 1, H, K))], axis=1)
            scale = jnp.sqrt(jnp.asarray(K, q_in.dtype))
            logits = jnp.einsum('bqhk,bthk->bhqt', qh, kh) / scale
            weights = jax.nn.softmax(logits, axis=-1)
            ctx = jnp.einsum('bhqt,bthk->bqhk', weights, vh).reshape(b, q_len, H * K)
            return ctx @ wo + bo

        def _forward(x, xf_1, xf_2, ln1_scale, ln1_offset, wq1, bq1, wk1, bk1, wv1, bv1, wo1, bo1, bias_k1, bias_v1, ln2_scale, ln2_offset, wq2, bq2, wk2, bk2, wv2, bv2, wo2, bo2, bias_k2, bias_v2, ln_mlp_scale, ln_mlp_offset, w_fc1, b_fc1, w_fc2, b_fc2):
            res = x
            h = _layer_norm(x, ln1_scale, ln1_offset)
            x = res + _cross_attention(h, xf_1, wq1, bq1, wk1, bk1, wv1, bv1, wo1, bo1, bias_k1, bias_v1)
            res = x
            h = _layer_norm(x, ln2_scale, ln2_offset)
            x = res + _cross_attention(h, xf_2, wq2, bq2, wk2, bk2, wv2, bv2, wo2, bo2, bias_k2, bias_v2)
            h = _layer_norm(x, ln_mlp_scale, ln_mlp_offset)
            h = jax.nn.gelu(h @ w_fc1 + b_fc1, approximate=False) @ w_fc2 + b_fc2
            return x + h
        return _forward(x, xf_1, xf_2, ln1_scale, ln1_offset, wq1, bq1, wk1, bk1, wv1, bv1, wo1, bo1, bias_k1, bias_v1, ln2_scale, ln2_offset, wq2, bq2, wk2, bk2, wv2, bv2, wo2, bo2, bias_k2, bias_v2, ln_mlp_scale, ln_mlp_offset, w_fc1, b_fc1, w_fc2, b_fc2)

    def _L3_xattn_ref(hidden_states, encoder_states, ltor_mask, cross_mask, ln1_s, ln1_b, w_qkv, b_qkv, w_ao, b_ao, ln2_s, ln2_b, w_q, b_q, w_kv, b_kv, w_co, b_co, ln3_s, ln3_b, w1, b1, w2, b2):
        import jax, jax.numpy as jnp
        import numpy as np
        H = 256
        NH = 16
        HD = H // NH
        EPS = 1e-05

        def gelu(x):
            return 0.5 * x * (1.0 + jnp.tanh(0.7978845608028654 * x * (1.0 + 0.044715 * x * x)))

        def layernorm(x, scale, bias):
            m = jnp.mean(x, axis=-1, keepdims=True)
            v = jnp.mean(jnp.square(x - m), axis=-1, keepdims=True)
            return (x - m) * jax.lax.rsqrt(v + EPS) * scale + bias

        def split_heads(x):
            b, s, _ = x.shape
            return x.reshape(b, s, NH, HD).transpose(0, 2, 1, 3)

        def merge_heads(x):
            b, nh, s, hd = x.shape
            return x.transpose(0, 2, 1, 3).reshape(b, s, nh * hd)

        def attention(q, k, v, mask):
            scores = jnp.einsum('bhqd,bhkd->bhqk', q, k) / jnp.sqrt(jnp.float32(HD))
            scores = scores * mask - 10000.0 * (1.0 - mask)
            probs = jax.nn.softmax(scores, axis=-1)
            return jnp.einsum('bhqk,bhkd->bhqd', probs, v)
        ln_out = layernorm(hidden_states, ln1_s, ln1_b)
        qkv = ln_out @ w_qkv + b_qkv
        q, k, v = jnp.split(qkv, 3, axis=-1)
        ctx = merge_heads(attention(split_heads(q), split_heads(k), split_heads(v), ltor_mask))
        attn_out = ctx @ w_ao + b_ao
        x = hidden_states + attn_out
        ln_out = layernorm(x, ln2_s, ln2_b)
        q = ln_out @ w_q + b_q
        kv = encoder_states @ w_kv + b_kv
        k, v = jnp.split(kv, 2, axis=-1)
        ctx = merge_heads(attention(split_heads(q), split_heads(k), split_heads(v), cross_mask))
        cross_out = ctx @ w_co + b_co
        x = x + cross_out
        ln_out = layernorm(x, ln3_s, ln3_b)
        mlp_out = gelu(ln_out @ w1 + b1) @ w2 + b2
        return x + mlp_out
    x = _L0_xattn_ref(x, ctx_2048, mask_BxS2_bf1, L0_xattn_ln1_w, L0_xattn_ln1_b, L0_xattn_q_w, L0_xattn_q_b, L0_xattn_k_w, L0_xattn_k_b, L0_xattn_v_w, L0_xattn_v_b, L0_xattn_cproj_w, L0_xattn_cproj_b, L0_xattn_ln2_w, L0_xattn_ln2_b, L0_xattn_fc_w, L0_xattn_fc_b, L0_xattn_proj_w, L0_xattn_proj_b)
    x = _L1_xattn_ref(ctx_2048, x, mask_BxS2_ik0, L1_xattn_q_w, L1_xattn_q_b, L1_xattn_kv_w, L1_xattn_kv_b, L1_xattn_out_w, L1_xattn_out_b, L1_xattn_postnorm_w, L1_xattn_mlp_w1, L1_xattn_mlp_b1, L1_xattn_mlp_w2, L1_xattn_mlp_b2)
    x = _L2_xattn_ref(x, ctx_2048, ctx_2048, L2_xattn_ln1_scale, L2_xattn_ln1_offset, L2_xattn_wq1, L2_xattn_bq1, L2_xattn_wk1, L2_xattn_bk1, L2_xattn_wv1, L2_xattn_bv1, L2_xattn_wo1, L2_xattn_bo1, L2_xattn_bias_k1, L2_xattn_bias_v1, L2_xattn_ln2_scale, L2_xattn_ln2_offset, L2_xattn_wq2, L2_xattn_bq2, L2_xattn_wk2, L2_xattn_bk2, L2_xattn_wv2, L2_xattn_bv2, L2_xattn_wo2, L2_xattn_bo2, L2_xattn_bias_k2, L2_xattn_bias_v2, L2_xattn_ln_mlp_scale, L2_xattn_ln_mlp_offset, L2_xattn_w_fc1, L2_xattn_b_fc1, L2_xattn_w_fc2, L2_xattn_b_fc2)
    x = _L3_xattn_ref(x, ctx_2048, mask_1x1xSxS2_fc1, mask_Bx1xSxS2_ff1, L3_xattn_ln1_s, L3_xattn_ln1_b, L3_xattn_w_qkv, L3_xattn_b_qkv, L3_xattn_w_ao, L3_xattn_b_ao, L3_xattn_ln2_s, L3_xattn_ln2_b, L3_xattn_w_q, L3_xattn_b_q, L3_xattn_w_kv, L3_xattn_b_kv, L3_xattn_w_co, L3_xattn_b_co, L3_xattn_ln3_s, L3_xattn_ln3_b, L3_xattn_w1, L3_xattn_b1, L3_xattn_w2, L3_xattn_b2)
    return x

_drawn_inputs = setup_inputs


def setup_inputs(seed=0):
    import zlib

    import numpy as np

    out = dict(_drawn_inputs(seed))
    spreads = {'L0_xattn_ln1_w': (1.0, 0.6),
     'L0_xattn_ln1_b': (0.0, 0.8),
     'L0_xattn_q_b': (0.0, 0.8),
     'L0_xattn_k_b': (0.0, 2.0),
     'L0_xattn_v_b': (0.0, 0.274),
     'L0_xattn_cproj_b': (0.0, 0.1),
     'L0_xattn_ln2_w': (1.0, 0.6),
     'L0_xattn_ln2_b': (0.0, 0.777),
     'L0_xattn_fc_b': (0.0, 0.1),
     'L0_xattn_proj_b': (0.0, 0.1),
     'L1_xattn_q_b': (0.0, 0.8),
     'L1_xattn_kv_b': (0.0, 0.8),
     'L1_xattn_out_b': (0.0, 0.8),
     'L1_xattn_postnorm_w': (1.0, 0.6),
     'L1_xattn_mlp_b1': (0.0, 0.1),
     'L1_xattn_mlp_b2': (0.0, 0.1),
     'L2_xattn_ln1_scale': (1.0, 0.6),
     'L2_xattn_ln1_offset': (0.0, 0.8),
     'L2_xattn_bq1': (0.0, 0.8),
     'L2_xattn_bk1': (0.0, 2.0),
     'L2_xattn_bv1': (0.0, 0.1),
     'L2_xattn_bo1': (0.0, 0.1),
     'L2_xattn_ln2_scale': (1.0, 0.6),
     'L2_xattn_ln2_offset': (0.0, 0.8),
     'L2_xattn_bq2': (0.0, 0.8),
     'L2_xattn_bk2': (0.0, 2.0),
     'L2_xattn_bv2': (0.0, 0.1),
     'L2_xattn_bo2': (0.0, 0.1),
     'L2_xattn_ln_mlp_scale': (1.0, 0.6),
     'L2_xattn_ln_mlp_offset': (0.0, 0.8),
     'L2_xattn_b_fc1': (0.0, 0.1),
     'L2_xattn_b_fc2': (0.0, 0.1),
     'L3_xattn_ln1_s': (1.0, 0.6),
     'L3_xattn_ln1_b': (0.0, 0.8),
     'L3_xattn_b_qkv': (0.0, 0.282),
     'L3_xattn_b_ao': (0.0, 0.1),
     'L3_xattn_ln2_s': (1.0, 0.6),
     'L3_xattn_ln2_b': (0.0, 2.0),
     'L3_xattn_b_q': (0.0, 2.0),
     'L3_xattn_b_kv': (0.0, 0.289),
     'L3_xattn_b_co': (0.0, 0.1),
     'L3_xattn_ln3_s': (1.0, 0.6),
     'L3_xattn_ln3_b': (0.0, 0.74),
     'L3_xattn_b1': (0.0, 0.1),
     'L3_xattn_b2': (0.0, 0.1)}
    factors = {'L0_xattn_q_w': 8.0,
     'L0_xattn_k_w': 8.0,
     'L1_xattn_q_w': 8.0,
     'L1_xattn_kv_w': 8.0,
     'L1_xattn_out_w': 8.0,
     'L2_xattn_wq1': 8.0,
     'L2_xattn_wk1': 8.0,
     'L2_xattn_bias_k1': 64.0,
     'L2_xattn_bias_v1': 64.0,
     'L2_xattn_wq2': 8.0,
     'L2_xattn_wk2': 8.0,
     'L2_xattn_bias_k2': 64.0,
     'L2_xattn_bias_v2': 64.0,
     'L3_xattn_w_q': 64.0}
    for name, (base, spread) in spreads.items():
        noise = np.random.default_rng([zlib.crc32(name.encode()), seed]).standard_normal(out[name].shape)
        drawn = base * np.exp(spread * noise) if base else spread * noise
        out[name] = jnp.asarray(drawn.astype(out[name].dtype))
    for name, factor in factors.items():
        out[name] = (out[name] * factor).astype(out[name].dtype)
    return out
```

```python
import numpy as np

import concourse.bass as bass
from concourse import mybir
from concourse.alu_op_type import AluOpType as ALU
from contextlib import ExitStack, contextmanager

F32 = mybir.dt.float32
ACT = mybir.ActivationFunctionType
AX = mybir.AxisListType

P = 128
B, S, D = 8, 128, 256
H, HD = 16, 16
HK = 128
F = 1024
G = 4
NG = B // G
NS = 2
SB = G // NS
T = SB * S
C = D // P
FC = F // P
HC = P // HD
BANK = 512
BIG = 3.4028234663852886e38

COLS = [("L0_ln1_w", 2), ("L0_ln1_b", 2), ("L0_q_b", 2), ("L0_k_b", 2), ("L0_v_b", 2), ("L0_ln2_w", 2),
        ("L0_ln2_b", 2), ("L0_fc_b", 8), ("L1_q_b", 2), ("L1_k_b", 2), ("L1_v_b", 2), ("L1_postnorm_w", 2),
        ("L1_mlp_b1", 8), ("L2_ln1_scale", 2), ("L2_ln1_offset", 2), ("L2_bq1", 16), ("L2_bk1", 16),
        ("L2_bias_k1", 16), ("L2_bias_v1", 16), ("L2_ln2_scale", 2), ("L2_ln2_offset", 2), ("L2_bq2", 16),
        ("L2_bk2", 16), ("L2_bias_k2", 16), ("L2_bias_v2", 16), ("L2_ln_mlp_scale", 2),
        ("L2_ln_mlp_offset", 2), ("L2_b_fc1", 8), ("L3_ln1_s", 2), ("L3_ln1_b", 2), ("L3_b_qkv", 6),
        ("L3_ln2_s", 2), ("L3_ln2_b", 2), ("L3_b_q", 2), ("L3_b_kv", 4), ("L3_ln3_s", 2), ("L3_ln3_b", 2),
        ("L3_b1", 8)]
NCOL = sum(n for _, n in COLS)
ROWS = ["L0_cproj_b", "L0_proj_b", "L1_out_b", "L1_mlp_b2", "L2_bo1", "L2_bo2", "L2_b_fc2", "L3_b_ao", "L3_b_co",
        "L3_b2"]


class Counter:

    def __init__(self, sem, base):
        self.sem, self.base, self.here = sem, base, 0


class Program:
    def __init__(self, nc, ctx, plan):
        self.nc, self.ctx, self.plan, self.found = nc, ctx, plan, {"seed": {}, "events": set()}
        self.engines = {"PE": nc.tensor, "ACT": nc.scalar, "DVE": nc.vector, "POOL": nc.gpsimd, "SP": nc.sync}
        self.counters, self.idle = {}, {}
        self.said = {}
        self.reached = {}
        self.turn, self.step = None, {}
        for name in ["PE", "ACT", "DVE", "POOL"] + list(plan.get("seed", {})):
            self.counter(name)

    def counter(self, name):
        if name not in self.counters:
            sem = self.ctx.enter_context(self.nc.semaphore(f"s_{name}"))
            seed = self.plan.get("seed", {}).get(name, 0)
            if seed:
                self.nc.sync.sem_inc(sem, seed)
            self.counters[name] = Counter(sem, seed)
        return self.counters[name]

    def say(self, name, instr, *events):
        c = self.counter(name)
        by = 1 if name in self.engines else 16
        instr.then_inc(c.sem, by)
        c.here += by
        for event in events:
            self.said[event] = (name, c.here, 0)
            self.found["events"].add(event)
        return instr

    def wait(self, engine, *events):
        most = {}
        for event in events:
            if event not in self.said:
                assert self.turn is None or event not in self.plan.get("events", ()), event
                continue
            name, value, back = self.said[event]
            value -= back * self.step.get(name, 0)
            most[name] = max(most.get(name, value), value)
        for name, value in most.items():
            if self.reached.get((engine, name), value - 1) >= value:
                continue
            self.reached[engine, name] = value
            c = self.counters[name]
            at = c.base + value
            if self.turn is not None and self.step.get(name, 0):
                at = self.turn * self.step[name] + at
            self.engines[engine].wait_ge(c.sem, at)
            if engine == "SP" and self.turn is not None:
                self.wait_ahead(engine)

    def wait_ahead(self, engine):
        if engine not in self.idle:
            self.idle[engine] = self.ctx.enter_context(self.nc.semaphore(f"idle_{engine}"))
        self.engines[engine].sem_inc(self.idle[engine], 1)

    def everyone(self, but=()):
        for name, c in self.counters.items():
            if name in but or not c.here:
                continue
            for engine in self.engines:
                if self.reached.get((engine, name), c.here - 1) < c.here:
                    self.engines[engine].wait_ge(c.sem, c.base + c.here)
        keep = {n for n in self.counters if n in but}
        self.said = {e: (n, v + 0, b) for e, (n, v, b) in self.said.items() if n in keep}
        for n, c in self.counters.items():
            if n not in keep:
                c.base, c.here = c.base + c.here, 0
        self.reached = {}

    @contextmanager
    def loop(self, name, turns, but=()):
        self.everyone(but)
        plan = self.plan.get(name, {"step": {}, "said": {}})
        self.step = plan["step"]
        for event, (n, v) in plan["said"].items():
            self.said[event] = (n, v, 1)
        with self.nc.Fori(0, turns) as turn:
            self.turn = turn
            yield turn
        step = {n: c.here for n, c in self.counters.items() if c.here and n not in but}
        assert not self.plan or plan["step"] == step, (name, plan["step"], step)
        self.found[name] = {"step": step, "said": {e: (n, v) for e, (n, v, b) in self.said.items() if not b and n not in but}}
        for n, v in step.items():
            self.found["seed"][n] = max(self.found["seed"].get(n, 0), v)
            self.counters[n].base += (turns - 1) * v
        self.turn, self.step, self.reached = None, {}, {}
        self.said = {e: (n, v, 0) for e, (n, v, b) in self.said.items() if not b}


def staged(n, stages, at=None):
    for t in range(n + max(lag for lag, _ in stages)):
        if at and t in at:
            at[t]()
        for lag, stage in stages:
            if 0 <= t - lag < n:
                stage(t - lag)


def build(nc, ins, out, plan):
    with ExitStack() as ctx:
        p = Program(nc, ctx, plan)
        say, wait = p.say, p.wait
        pe, act, dve, pool, sp = nc.tensor, nc.scalar, nc.vector, nc.gpsimd, nc.sync

        def sb(name, shape, where=ctx):
            return where.enter_context(nc.sbuf_tensor(name, shape, F32))

        psum = ctx.enter_context(nc.psum_tensor("psum", [P, 8, BANK], F32))

        def bank(k):
            return psum[:, k, :]

        ident = sb("ident", [P, P])
        of_head = sb("of_head", [P, HC])
        cols = sb("cols", [P, NCOL])
        col_rows = sb("col_rows", [P, 2, P])
        rows = sb("rows", [P, len(ROWS), D])
        half = sb("half", [P, SB])
        weights = sb("weights", [P, 12288])
        x_all = sb("x_all", [P, B, D])
        ctxT_all = sb("ctxT_all", [P, C, B * S])
        hT_all = sb("hT_all", [P, C, B * S])

        col, at = {}, 0
        for name, n in COLS:
            col[name] = cols[:, at:at + n]
            at += n

        def row(name):
            return rows[:, ROWS.index(name), :]

        for k in range(2):
            n = min(P, NCOL - k * P)
            say("dma_setup", sp.dma_start(col_rows[0:n, k, :], ins["cols"][k * P:k * P + n, :]), "cols loaded")

        w = {}

        def load_weights(*groups):
            at = 0
            for counter, names in groups:
                for name in names:
                    k, n = ins[name].shape
                    w[name] = weights[:, at:at + k // P * n].rearrange("p (c n) -> p c n", n=n)
                    at += k // P * n
                    say(counter, sp.dma_start(w[name], ins[name].rearrange("(c p) n -> p c n", p=P)), counter)

        pool.memset(half[:, :], -0.5)
        say("POOL", pool.memset(ident[:, :], 0.0), "ident cleared")
        say("POOL", pool.memset(of_head[:, :], 1.0), "of_head filled")
        wait("POOL", "ident cleared")
        say("POOL", pool.affine_select(out=ident[:, :], in_=ident[:, :], compare_op=ALU.not_equal, fill=1.0,
                                       base=0, pattern=[[-1, P]], channel_multiplier=1), "ident made")
        wait("POOL", "of_head filled")
        say("POOL", pool.affine_select(out=of_head[:, :], in_=of_head[:, :], compare_op=ALU.is_ge, fill=0.0, base=0,
                                       pattern=[[-HD, HC]], channel_multiplier=1), "of_head cut below")
        wait("POOL", "of_head cut below")
        say("POOL", pool.affine_select(out=of_head[:, :], in_=of_head[:, :], compare_op=ALU.is_ge, fill=0.0, base=HD - 1,
                                       pattern=[[HD, HC]], channel_multiplier=-1), "of_head made")
        wait("PE", "ident made")
        wait("PE", "cols loaded")
        for k in range(2):
            n = min(P, NCOL - k * P)
            say("PE", pe.transpose(bank(1)[:, k * P:k * P + n], col_rows[0:n, k, :], ident[0:n, 0:n]), "cols turned")
        wait("DVE", "cols turned")
        say("DVE", dve.tensor_copy(cols[:, :], bank(1)[:, 0:NCOL]), "cols made")
        wait("DVE", "cols made")
        scale16 = float(1.0 / np.sqrt(np.float32(HD)))
        scaleK = float(1.0 / np.sqrt(np.float32(HK)))
        scale_of = {"L0_q_b": scale16, "L1_q_b": 1.0 / HD, "L3_b_q": scale16, "L2_bq1": scaleK, "L2_bq2": scaleK}
        for name, scale in scale_of.items():
            dve.tensor_scalar(col[name], col[name], scale, None, ALU.mult)
        dve.tensor_scalar(col["L3_b_qkv"][:, 0:C], col["L3_b_qkv"][:, 0:C], scale16, None, ALU.mult)
        for j in "12":
            say("DVE", dve.tensor_tensor(col["L2_bk" + j], col["L2_bk" + j], col["L2_bias_k" + j], ALU.subtract), "cols made")

        lin = {"bank": 0, "engine": 0}

        def next_bank(of):
            lin["bank"] += 1
            return of[lin["bank"] % len(of)]

        def next_engine():
            lin["engine"] += 1
            return ("ACT", "DVE")[lin["engine"] % 2]

        ALL = tuple(range(8))
        UPPER = (4, 5, 6, 7)

        def affine(e, dst, src, scale, bias, *events):
            if e == "ACT":
                i = act.activation(dst, src, ACT.Identity, bias=0.0 if bias is None else bias,
                                   scale=1.0 if scale is None else scale)
            elif bias is None:
                i = dve.tensor_scalar(dst, src, 1.0 if scale is None else scale, None, ALU.mult)
            elif scale is None:
                i = dve.tensor_scalar(dst, src, bias, None, ALU.add)
            else:
                i = dve.tensor_scalar(dst, src, scale, bias, ALU.mult, ALU.add)
            say(e, i, *events)

        def norm(tag, x, batches, xn, st, rms=False):
            eps = 1e-6 if rms else 1e-5
            lo, hi = batches[0], batches[-1] + 1
            mean = st["mv"][:, lo:hi, 0]
            var = st["mv"][:, lo:hi, 1]
            wait("DVE", tag + "x ready")
            for b in batches:
                say("DVE", dve.bn_stats(st["bn"][:, 6 * b:6 * b + 6], x[:, b, :]), tag + "stats")
            wait("DVE", tag + "stats", tag + "ve read")
            p.wait_ahead("DVE")
            for b in batches:
                say("DVE", dve.bn_aggr(st["mv"][:, b, :], st["bn"][:, 6 * b:6 * b + 6]), tag + "moments")
            wait("DVE", tag + "moments")
            if rms:
                say("DVE", dve.tensor_tensor(st["ve"][:, lo:hi], mean, mean, ALU.mult), tag + "mean squared")
                wait("DVE", tag + "mean squared")
                say("DVE", dve.scalar_tensor_tensor(out=st["ve"][:, lo:hi], in0=st["ve"][:, lo:hi], scalar=eps, in1=var,
                                                    op0=ALU.add, op1=ALU.add), tag + "ve")
            else:
                say("DVE", dve.tensor_scalar(st["ve"][:, lo:hi], var, eps, None, ALU.add), tag + "ve")
            wait("POOL", tag + "ve")
            say("POOL", pool.tensor_tensor(st["rstd"][:, lo:hi], st["ve"][:, lo:hi], half[:, 0:hi - lo], ALU.pow),
                tag + "rstd", tag + "ve read")
            wait("DVE", tag + "rstd", tag + "xn turned")
            for b in batches:
                if rms:
                    i = dve.tensor_scalar(xn[:, b, :], x[:, b, :], st["rstd"][:, b:b + 1], None, ALU.mult)
                else:
                    i = dve.tensor_scalar(xn[:, b, :], x[:, b, :], st["mv"][:, b, 0:1], st["rstd"][:, b:b + 1],
                                          ALU.subtract, ALU.mult)
                say("DVE", i, tag + "xn ready", tag + "x normed")

        def to_features(src, ready, turned, dst, dst_ready, dst_free, scale=None, bias=None, banks=ALL, also=None,
                        engine=None):
            k = next_bank(banks)
            wait("PE", ready, f"bank {k} drained")
            for c in range(C):
                for b in range(SB):
                    i = pe.transpose(bank(k)[:, (c * SB + b) * P:(c * SB + b + 1) * P], src[:, b, c * P:(c + 1) * P], ident[:, :])
            say("PE", i, f"bank {k} filled", turned)
            e = engine or next_engine()
            wait(e, f"bank {k} filled", *dst_free)
            for c in range(C):
                affine(e, dst[:, c, :], bank(k)[:, c * T:(c + 1) * T], None if scale is None else scale[:, c:c + 1],
                       None if bias is None else bias[:, c:c + 1], dst_ready, f"bank {k} drained")
            if also is not None:
                affine(e, also, bank(k).rearrange("p (c t) -> p c t", c=C), None, None, f"bank {k} drained")

        def linear_features(wt, src, ready, used, n_out, drain, banks=ALL):
            for m in range(0, n_out, 2):
                k = next_bank(banks)
                wait("PE", ready, f"bank {k} drained")
                for n in range(2):
                    for c in range(C):
                        i = pe.matmul(bank(k)[:, n * T:(n + 1) * T], wt[:, c, (m + n) * P:(m + n + 1) * P], src[:, c, :],
                                      start=c == 0, stop=c == C - 1)
                say("PE", i, f"bank {k} filled", used)
                drain(m, k)

        def linear_tokens(wt, src, ready, used, banks=ALL):
            k = next_bank(banks)
            wait("PE", ready, f"bank {k} drained")
            for b in range(SB):
                for c in range(C):
                    i = pe.matmul(bank(k)[:, b * D:(b + 1) * D], src[:, c, b * P:(b + 1) * P], wt[:, c, :],
                                  start=c == 0, stop=c == C - 1)
            say("PE", i, f"bank {k} filled", used)
            return k

        class Stream:

            def __init__(self, t, where, n_src):
                def b(name, shape):
                    return sb(t + name, shape, where)
                self.t, self.n_src = t, n_src
                self.x, self.xb, self.xn = (b(n, [P, SB, D]) for n in ("x", "xb", "xn"))
                self.hT, self.cT, self.qT = (b(n, [P, C, T]) for n in ("hT", "cT", "qT"))
                self.kT = b("kT", [P, C, n_src, T])
                self.qm = b("qm", [P, C, HC, T])
                self.vaug = b("vaug", [P, n_src, SB, H, HD + 1])
                self.OT = b("OT", [P, SB, C, P])
                self.aT = self.qm[:, 0, :, :]
                self.on = b("on", [P, D])
                self.rec = b("rec", [P, H])
                self.st = {"bn": b("bn", [P, 6 * SB]), "mv": b("mv", [P, SB, 2]), "ve": b("ve", [P, SB]), "rstd": b("rstd", [P, SB])}
                say("POOL", pool.memset(self.vaug[:, :, :, :, HD:HD + 1], 1.0), "ones set")

            def norm(self, x=None, batches=range(SB), rms=False):
                norm(self.t, self.x if x is None else x, list(batches), self.xn, self.st, rms)

            def normed_features(self, scale, bias, banks=ALL):
                t = self.t
                to_features(self.xn, t + "xn ready", t + "xn turned", self.hT, t + "hT ready", [t + "hT used"], scale, bias, banks)

            def residual(self, name):
                t = self.t
                wait("POOL", t + "x ready", t + "xb used", t + "x normed")
                say("POOL", pool.tensor_tensor(self.xb[:, :, :], self.x[:, :, :],
                                               row(name).unsqueeze(1).to_broadcast([P, SB, D]), ALU.add), t + "xb ready", t + "x copied")

            def queries(self, wt, bias, scale, banks=ALL):
                t = self.t

                def drain(m, k):
                    wait("DVE", f"bank {k} filled", t + "qT used")
                    for n in range(2):
                        affine("DVE", self.qT[:, n, :], bank(k)[:, n * T:(n + 1) * T], scale, bias[:, n:n + 1],
                               t + "qT ready", f"bank {k} drained")
                    for n, e in enumerate(("ACT", "DVE")):
                        wait(e, t + "qT ready", t + "qm used", t + "aT used")
                        for j in range(HC):
                            affine(e, self.qm[:, n, j, :], self.qT[:, n, :], of_head[:, j:j + 1], None, t + f"qm {n} ready", t + "qT used")
                linear_features(wt, self.hT, t + "hT ready", t + "hT used", C, drain, banks)

            def keys(self, wt, bias, src, ready, used, s, banks=ALL):
                t = self.t

                def drain(m, k):
                    e = next_engine()
                    wait(e, f"bank {k} filled", t + "kT used")
                    for n in range(2):
                        affine(e, self.kT[:, n, s, :], bank(k)[:, n * T:(n + 1) * T], None, bias[:, n:n + 1], t + f"kT {s} ready",
                               f"bank {k} drained")
                linear_features(wt, src, ready, used, C, drain, banks)

            def values(self, wt, src, ready, used, s, banks=ALL):
                t = self.t
                k = linear_tokens(wt, src, ready, used, banks)
                wait("ACT", f"bank {k} filled", t + "vaug used")
                affine("ACT", self.vaug[:, s, :, :, 0:HD].rearrange("p b h d -> p (b h) d"),
                       bank(k).rearrange("p (g d) -> p g d", d=HD), None, None, t + "vaug ready", f"bank {k} drained")

            def mlp_up(self, w1, b1, func):
                t = self.t

                def drain(m, k):
                    wait("ACT", f"bank {k} filled", t + "aT used", t + "qm used")
                    for n in range(2):
                        say("ACT", act.activation(self.aT[:, m + n, :], bank(k)[:, n * T:(n + 1) * T], func,
                                                  bias=b1[:, m + n:m + n + 1]), t + "aT ready", f"bank {k} drained")
                linear_features(w1, self.hT, t + "hT ready", t + "hT used", FC, drain)

            def mlp_down(self, w2):
                t = self.t
                k = next_bank(ALL)
                wait("PE", t + "aT ready", f"bank {k} drained")
                for b in range(SB):
                    for c in range(FC):
                        i = pe.matmul(bank(k)[:, b * D:(b + 1) * D], self.aT[:, c, b * P:(b + 1) * P], w2[:, c, :],
                                      start=c == 0, stop=c == FC - 1)
                say("PE", i, f"bank {k} filled", t + "aT used")
                wait("DVE", f"bank {k} filled", t + "xb ready", t + "x copied", t + "x turned", t + "x stored")
                say("DVE", dve.tensor_tensor(self.x[:, :, :], bank(k).rearrange("p (b d) -> p b d", b=SB), self.xb[:, :, :],
                                             ALU.add), t + "x ready", t + "xb used", f"bank {k} drained")

        def attention(streams, sh, n_src, mask_stage, v_bias, w_out, into_xb, after, at):
            per = 8 // n_src
            nk = n_src * S
            n_batch = H // per
            units = [(s, b, k * per // HC, k * per % HC, k % 2) for s in streams for b in range(SB) for k in range(n_batch)]

            def drained(r):
                return f"bank {2 * r} drained", f"bank {2 * r + 1} drained"

            def scores(u):
                s, b, c, h0, r = units[u]
                wait("PE", s.t + f"qm {c} ready", *(s.t + f"kT {n} ready" for n in range(n_src)), *drained(r))
                both = psum[:, 2 * r:2 * r + 2, :].rearrange("p g k -> p (g k)")
                for n in range(per):
                    i = pe.matmul(both[:, n * nk:(n + 1) * nk], s.qm[:, c, h0 + n, b * S:(b + 1) * S],
                                  s.kT[:, c, 0:n_src, b * S:(b + 1) * S], start=True, stop=True)
                say("PE", i, f"banks {r} scored", s.t + "qm used", s.t + "kT used")

            def softmax(u):
                s, b, _, _, r = units[u]
                v = u % len(sh["tiles"])
                tile = sh["tiles"][v]
                tv = tile[:, :].rearrange("p (h k) -> p h k", k=nk)
                sc = psum[:, 2 * r:2 * r + 2, :].rearrange("p g (h k) -> p (g h) k", k=nk)
                wait("DVE", f"banks {r} scored", f"tile {v} turned")
                mask_stage(s, b, sc, tv, per, nk, v, drained(r))
                mx = sh["max"][:, u % 2, 0:per]
                wait("DVE", f"tile {v} masked", f"max {u % 2} used")
                say("DVE", dve.tensor_reduce(mx, tv, AX.X, ALU.max), f"max {u % 2}")
                wait("POOL", f"max {u % 2}")
                say("POOL", pool.tensor_tensor(tv, tv, mx.unsqueeze(2).to_broadcast([P, per, nk]), ALU.subtract),
                    f"tile {v} shifted", f"max {u % 2} used")
                wait("ACT", f"tile {v} shifted")
                say("ACT", act.activation(tile[:, :], tile[:, :], ACT.Exp), f"tile {v} exp")

            def turn(u):
                v = u % len(sh["tiles"])
                for n in range(2):
                    wait("PE", f"tile {v} exp", f"bank {4 + n} drained")
                    for q in range(4):
                        i = pe.transpose(bank(4 + n)[:, q * P:(q + 1) * P], sh["tiles"][v][:, (4 * n + q) * P:(4 * n + q + 1) * P], ident[:, :])
                    say("PE", i, f"bank {4 + n} filled", f"tile {v} turned")
                    wait("ACT", f"bank {4 + n} filled", f"PT {u % 2} used")
                    say("ACT", act.copy(sh["PT"][:, u % 2, n, :], bank(4 + n)), f"PT {u % 2} {n} ready", f"bank {4 + n} drained")

            def weigh(u):
                s, b, c, h0, _ = units[u]
                if u % n_batch == 0:
                    wait("PE", "bank 6 drained")
                for n in range(per):
                    h = HC * c + h0 + n
                    for src in range(n_src):
                        q = n * n_src + src
                        wait("PE", f"PT {u % 2} {q // 4} ready", s.t + "vaug ready")
                        i = pe.matmul(bank(6)[:, h * 17:(h + 1) * 17], sh["PT"][:, u % 2, q // 4, (q % 4) * P:(q % 4 + 1) * P],
                                      s.vaug[:, src, b, h, :], start=src == 0, stop=src == n_src - 1)
                say("PE", i, "bank 6 filled", f"PT {u % 2} used", s.t + "vaug used")

            def last(stage):
                return lambda u: stage(*units[u][0:2]) if u % n_batch == n_batch - 1 else None

            def divide(s, b):
                t = s.t
                ov = bank(6)[:, 0:H * 17].rearrange("p (h d) -> p h d", d=17)
                wait("DVE", "bank 6 filled", t + "on turned")
                say("DVE", dve.reciprocal(s.rec[:, :].unsqueeze(2), ov[:, :, 16:17]), t + "rec")
                wait("DVE", t + "rec")
                say("DVE", dve.tensor_tensor(s.on[:, :].rearrange("p (h d) -> p h d", d=HD), ov[:, :, 0:HD],
                                             s.rec[:, :].unsqueeze(2).to_broadcast([P, H, HD]), ALU.mult), t + "on ready", "bank 6 drained")

            def features(s, b):
                t = s.t
                wait("PE", t + "on ready", "bank 7 drained")
                for c in range(C):
                    i = pe.transpose(bank(7)[:, c * P:(c + 1) * P], s.on[:, c * P:(c + 1) * P], ident[:, :])
                say("PE", i, "bank 7 filled", t + "on turned")
                wait("DVE", "bank 7 filled", t + f"OT {b} used")
                for c in range(C):
                    affine("DVE", s.OT[:, b, c, :], bank(7)[:, c * P:(c + 1) * P], None, v_bias[:, c:c + 1], t + f"OT {b} ready", "bank 7 drained")

            def project(s, b):
                t = s.t
                wait("PE", t + f"OT {b} ready", "bank 7 drained")
                for c in range(C):
                    i = pe.matmul(bank(7)[:, 0:D], s.OT[:, b, c, :], w_out[:, c, :], start=c == 0, stop=c == C - 1)
                say("PE", i, "bank 7 filled", t + f"OT {b} used")
                wait("DVE", "bank 7 filled", t + "xb ready", *([] if into_xb else [t + "x copied", t + "x turned"]))
                say("DVE", dve.tensor_tensor((s.xb if into_xb else s.x)[:, b, :], bank(7)[:, 0:D], s.xb[:, b, :], ALU.add),
                    t + "x ready", t + "xb used", "bank 7 drained")
                after(s, b)

            staged(len(units), [(2, turn), (0, scores), (0, softmax), (3, weigh), (3, last(divide)), (4, last(features)),
                                (5, last(project))], at)

        def shared_buffers(where, t):
            return {"tiles": [sb(f"{t}tile{k}", [P, 2 * BANK], where) for k in range(3)],
                    "PT": sb(t + "PT", [P, 2, 2, BANK], where), "max": sb(t + "max", [P, 2, 8], where)}

        def block(streams, sh, project_in, n_src, mask_stage, v_bias, w_out, row_out, into_xb, rms, scale_bias, mlp):
            for s in streams:
                s.residual(row_out)
            project_in(streams[0], ALL)
            attention(streams, sh, n_src, mask_stage, v_bias, w_out, into_xb,
                      lambda s, b: s.norm(s.xb if into_xb else s.x, [b], rms), {2: lambda: project_in(streams[1], UPPER)})
            if mlp is not None:
                run_mlp(streams, scale_bias, *mlp)

        def run_mlp(streams, scale_bias, w1, b1, func, w2, row_out):
            first, second = streams
            for s in streams:
                s.residual(row_out)
            first.normed_features(*scale_bias)
            first.mlp_up(w1, b1, func)
            second.normed_features(*scale_bias)
            first.mlp_down(w2)
            second.mlp_up(w1, b1, func)
            second.mlp_down(w2)

        with ExitStack() as scope:
            streams = [Stream(f"A{k} ", scope, 2) for k in range(NS)]
            sh = shared_buffers(scope, "A ")
            m0 = sb("m0", [P, B, S], scope)
            m1 = sb("m1", [P, B, 2, S], scope)
            m0_raw = sh["tiles"][0][:, 0:B * S // 4].bitcast(mybir.dt.uint8)
            m1_raw = sh["tiles"][1][:, :].bitcast(mybir.dt.int32)
            say("dma_setup2", sp.dma_start(m0_raw, ins["mask_bf1"].partition_broadcast(P)), "key masks loaded")
            say("dma_setup2", sp.dma_start(m1_raw, ins["mask_ik0"].partition_broadcast(P)), "key masks loaded")
            say("dma_setup2", sp.dma_start(rows[:, :, :].rearrange("p a b -> p (a b)"), ins["rows"].partition_broadcast(P)),
                "key masks loaded")
            load_weights(("L0 attention weights", ("L0_q_w", "L0_k_w", "L0_v_w", "L0_cproj_w")),
                         ("L0 MLP weights", ("L0_fc_w", "L0_proj_w")),
                         ("L1 weights", ("L1_q_w", "L1_k_w", "L1_v_w", "L1_out_w", "L1_mlp_w1", "L1_mlp_w2")))
            say("POOL", pool.memset(m1[:, :, 1, :], 0.0), "m1 cleared")
            wait("DVE", "key masks loaded")
            dve.tensor_scalar(m0[:, :, :].rearrange("p b s -> p (b s)"), m0_raw, 0.0, -BIG, ALU.is_equal, ALU.mult)
            say("DVE", dve.tensor_scalar(m1[:, :, 0, :], m1_raw.rearrange("p (b s) -> p b s", b=B), 0.0, -BIG, ALU.is_equal,
                                         ALU.mult), "masks made")

            late = ("L0 attention weights", "L0 MLP weights", "L1 weights")
            with p.loop("A", NG, but=late) as turn:
                for k, s in enumerate(streams):
                    wait("SP", s.t + "x ready", s.t + "x stored", s.t + "x copied", s.t + "x normed", s.t + "x turned", s.t + "xn turned")
                    for name, dst in (("x", s.x), ("ctx", s.xn)):
                        say(f"dma_{name}{k}", sp.dma_start(dst[:, :, :], ins[name].rearrange("b s d -> s b d")[:, bass.ds(turn * G + k * SB, SB), :]),
                            s.t + {"x": "x ready", "ctx": "ctx loaded"}[name])
                for k, s in enumerate(streams):
                    to_features(s.xn, s.t + "ctx loaded", s.t + "xn turned", s.cT, s.t + "cT ready", [s.t + "cT used"], engine="DVE",
                                also=ctxT_all[:, :, bass.ds(turn * G * S + k * T, T)])
                    s.norm()

                def key_mask(mask, n):
                    def stage(s, b, sc, tv, per, nk, v, drained):
                        i = turn * G + streams.index(s) * SB + b
                        mb = mask[:, bass.ds(i, 1), :].to_broadcast([P, per, nk])
                        say("DVE", dve.tensor_tensor(tv, sc, mb, ALU.add), f"tile {v} masked", *drained)
                    return stage

                def project_in0(s, banks):
                    t = s.t
                    wait("PE", "L0 attention weights")
                    s.normed_features(col["L0_ln1_w"], col["L0_ln1_b"], banks)
                    s.queries(w["L0_q_w"], col["L0_q_b"], scale16, banks)
                    s.keys(w["L0_k_w"], col["L0_k_b"], s.cT, t + "cT ready", t + "cT used", 0, banks)
                    s.values(w["L0_v_w"], s.cT, t + "cT ready", t + "cT used", 0, banks)

                block(streams, sh, project_in0, 1, key_mask(m0, 1), col["L0_v_b"], w["L0_cproj_w"], "L0_cproj_b", False, False,
                      None, None)
                wait("PE", "L0 MLP weights")
                run_mlp(streams, (col["L0_ln2_w"], col["L0_ln2_b"]), w["L0_fc_w"], col["L0_fc_b"], ACT.Gelu_apprx_tanh,
                        w["L0_proj_w"], "L0_proj_b")

                def project_in1(s, banks):
                    t = s.t
                    wait("PE", "L1 weights")
                    to_features(s.x, t + "x ready", t + "x turned", s.hT, t + "hT ready", [t + "hT used"], banks=banks)
                    s.queries(w["L1_q_w"], col["L1_q_b"], 1.0 / HD, banks)
                    for n, (src, name) in enumerate(((s.cT, "cT"), (s.hT, "hT"))):
                        s.keys(w["L1_k_w"], col["L1_k_b"], src, f"{t}{name} ready", f"{t}{name} used", n, banks)
                        s.values(w["L1_v_w"], src, f"{t}{name} ready", f"{t}{name} used", n, banks)

                block(streams, sh, project_in1, 2, key_mask(m1[:, :, :, :].rearrange("p b n s -> p b (n s)"), 2), col["L1_v_b"],
                      w["L1_out_w"], "L1_out_b", True, True, (col["L1_postnorm_w"], None),
                      (w["L1_mlp_w1"], col["L1_mlp_b1"], ACT.Gelu_apprx_tanh, w["L1_mlp_w2"], "L1_mlp_b2"))

                for k, s in enumerate(streams):
                    t = s.t
                    s.norm()
                    to_features(s.xn, t + "xn ready", t + "xn turned", hT_all[:, :, bass.ds(turn * G * S + k * T, T)], t + "hT_all", [],
                                col["L2_ln1_scale"], col["L2_ln1_offset"], engine="DVE")
                    wait("POOL", t + "x ready")
                    p.wait_ahead("POOL")
                    say("POOL", pool.tensor_tensor(x_all[:, bass.ds(turn * G + k * SB, SB), :], s.x[:, :, :],
                                                   row("L2_bo1").unsqueeze(1).to_broadcast([P, SB, D]), ALU.add), t + "x stored")

        p.everyone()
        load_weights(("weights C", ("L2_w_fc1", "L2_w_fc2", "L3_w_qkv", "L3_w_ao", "L3_w_q", "L3_w_kv", "L3_w_co", "L3_w1", "L3_w2")))

        with ExitStack() as scope:
            NP_ = H // 2

            def b2(name, shape):
                return sb(f"B {name}", shape, scope)
            wq = [b2(f"wq{k}", [P, C, HK]) for k in range(2)]
            wk = [b2(f"wk{k}", [P, C, HK]) for k in range(2)]
            wv = b2("wv", [P, C, 2 * HK])
            wo = b2("wo", [P, 2, D])
            qT = [b2(f"qT{k}", [P, B * S]) for k in range(2)]
            kT = [b2(f"kT{k}", [P, B * S]) for k in range(2)]
            vv = b2("v", [P, B, 2 * HK])
            tiles = [b2(f"tile{k}", [P, B * S]) for k in range(2)]
            PT = b2("PT", [P, 2, 2, BANK])
            OT = [b2(f"OT{k}", [P, B * S]) for k in range(2)]
            st2 = {n: b2(n, [P, 2, B]) for n in ("max", "own", "sum", "rec")}
            bv = b2("bv", [P, H * HK])
            bias_v = b2("bias_v", [P, H * HK])
            bcol = b2("bcol", [P, 2, 2])
            bvcol = b2("bvcol", [P, 2])
            norm_st = [{n: b2(n + str(k), shape) for n, shape in (("bn", [P, 6 * SB]), ("mv", [P, SB, 2]), ("ve", [P, SB]), ("rstd", [P, SB]))}
                       for k in range(2)]
            xs = [b2(f"xs{k}", [P, SB, D]) for k in range(2)]
            xn = [b2(f"xn{k}", [P, SB, D]) for k in range(2)]

            def cross_attention(j):
                def load_qk(k, head):
                    for n, (dst, name) in enumerate(((wq[k], f"wq{j}"), (wk[k], f"wk{j}"))):
                        wait("SP", f"{'qk'[n]} {k} projected")
                        say(f"dma_w{'qk'[n]}{k}", sp.dma_start(dst[:, :, :], ins[name].rearrange("(c p) n -> p c n", p=P)[:, :, bass.ds(head * HK, HK)]),
                            f"w{'qk'[n]} {k} loaded")
                    wait("POOL", f"q {k} ready", f"k {k} ready")
                    p.wait_ahead("POOL")
                    pool.tensor_copy(bcol[:, k, 0:1], col[f"L2_bq{j}"][:, bass.ds(head, 1)])
                    say("POOL", pool.tensor_copy(bcol[:, k, 1:2], col[f"L2_bk{j}"][:, bass.ds(head, 1)]), f"bias {k} ready")

                def load_vo(turn):
                    wait("SP", "v projected")
                    say("dma_wv", sp.dma_start(wv[:, :, :], ins[f"wv{j}"].rearrange("(c p) n -> p c n", p=P)[:, :, bass.ds(turn * 2 * HK, 2 * HK)]),
                        "wv loaded")

                def load_o(turn):
                    wait("SP", "out projected")
                    say("dma_wo", sp.dma_start(wo[:, :, :], ins[f"wo{j}"].rearrange("(h p) n -> p h n", p=P)[:, bass.ds(turn * 2, 2), :]),
                        "wo loaded")

                def load_bias_v(turn):
                    wait("POOL", "OT 0 ready", "OT 1 ready")
                    p.wait_ahead("POOL")
                    say("POOL", pool.tensor_copy(bvcol[:, :], col[f"L2_bias_v{j}"][:, bass.ds(turn * 2, 2)]), "bias_v ready")

                def project(kind, k, slot, banks):
                    wt, src, dst = {"q": (wq, hT_all, qT), "k": (wk, ctxT_all, kT)}[kind]
                    wait("PE", f"w{kind} {k} loaded", *(f"bank {b} drained" for b in banks))
                    for n in range(2):
                        for c in range(C):
                            i = pe.matmul(bank(banks[n]), wt[k][:, c, :], src[:, c, n * BANK:(n + 1) * BANK], start=c == 0, stop=c == C - 1)
                    say("PE", i, f"bank {banks[0]} filled", f"{kind} {k} projected")
                    e = {"q": "DVE", "k": "ACT"}[kind]
                    wait(e, f"bank {banks[0]} filled", f"bias {k} ready", f"head {slot} scored")
                    affine(e, dst[slot][:, :], psum[:, banks[0]:banks[0] + 2, :].rearrange("p a b -> p (a b)"),
                           scaleK if kind == "q" else None, bcol[:, k, 0:1] if kind == "q" else bcol[:, k, 1:2],
                           f"{kind} {k} ready", *(f"bank {b} drained" for b in banks))

                def values(n, turn, b_):
                    wait("PE", "wv loaded", f"bank {b_} drained")
                    for k in range(2):
                        for c in range(C):
                            i = pe.matmul(bank(b_)[:, k * 2 * HK:(k + 1) * 2 * HK], ctxT_all[:, c, (2 * n + k) * S:(2 * n + k + 1) * S],
                                          wv[:, c, :], start=c == 0, stop=c == C - 1)
                    say("PE", i, f"bank {b_} filled", "v projected")
                    wait("DVE", f"bank {b_} filled", "v 1 weighed")
                    say("DVE", dve.tensor_tensor(vv[:, 2 * n:2 * n + 2, :], bank(b_).rearrange("p (k d) -> p k d", k=2),
                                                 bv[:, bass.ds(turn * 2 * HK, 2 * HK)].unsqueeze(1).to_broadcast([P, 2, 2 * HK]), ALU.add),
                        f"bank {b_} drained", "v ready")

                def scores(h):
                    wait("PE", f"q {1 - h} ready", f"k {1 - h} ready", f"bank {2 * h} drained", f"bank {2 * h + 1} drained")
                    for b in range(B):
                        i = pe.matmul(bank(2 * h + b // 4)[:, (b % 4) * S:(b % 4 + 1) * S], qT[h][:, b * S:(b + 1) * S],
                                      kT[h][:, b * S:(b + 1) * S], start=True, stop=True)
                    say("PE", i, f"bank {2 * h} filled", f"head {h} scored")

                def softmax(h):
                    mx, own, total, rec = (st2[n][:, h, :] for n in ("max", "own", "sum", "rec"))
                    sc = psum[:, 2 * h:2 * h + 2, :].rearrange("p a (b k) -> p (a b) k", k=S)
                    tv = tiles[h][:, :].rearrange("p (b k) -> p b k", k=S)
                    over = [P, B, S]
                    wait("DVE", f"bank {2 * h} filled", f"own {h} ready")
                    say("DVE", dve.tensor_reduce(mx, sc, AX.X, ALU.max), f"keys' max {h}")
                    wait("DVE", f"keys' max {h}")
                    say("DVE", dve.tensor_scalar(mx, mx, 0.0, None, ALU.max), f"max {h} ready")
                    wait("DVE", f"max {h} ready", f"tile {h} turned")
                    say("DVE", dve.tensor_tensor(tv, sc, mx.unsqueeze(2).to_broadcast(over), ALU.subtract), f"tile {h} shifted",
                        f"bank {2 * h} drained", f"bank {2 * h + 1} drained")
                    wait("ACT", f"tile {h} shifted", f"sum {h} ready")
                    say("ACT", act.activation(own, mx, ACT.Exp, scale=-1.0), f"own {h} ready")
                    say("ACT", act.activation(tiles[h][:, :], tiles[h][:, :], ACT.Exp), f"tile {h} exp")
                    wait("DVE", f"tile {h} exp")
                    say("DVE", dve.tensor_reduce(total, tv, AX.X, ALU.add), f"keys' sum {h}")
                    wait("DVE", f"keys' sum {h}")
                    say("DVE", dve.tensor_tensor(total, total, own, ALU.add), f"sum {h} ready")
                    wait("DVE", f"sum {h} ready", f"tile {h} divided")
                    say("DVE", dve.reciprocal(rec, total), f"rec {h} ready")
                    wait("POOL", f"rec {h} ready")
                    say("POOL", pool.tensor_tensor(tv, tv, rec.unsqueeze(2).to_broadcast(over), ALU.mult), f"tile {h} divided")

                def turn_weights(h):
                    for n in range(2):
                        wait("PE", f"tile {h} divided", f"bank {4 + n} drained")
                        for k in range(4):
                            i = pe.transpose(bank(4 + n)[:, k * P:(k + 1) * P], tiles[h][:, (4 * n + k) * P:(4 * n + k + 1) * P], ident[:, :])
                        say("PE", i, f"bank {4 + n} filled", f"tile {h} turned")
                        wait("ACT", f"bank {4 + n} filled", f"v {h} weighed")
                        say("ACT", act.copy(PT[:, h, n, :], bank(4 + n)), f"PT {h} {n} ready", f"bank {4 + n} drained")

                def weigh(h):
                    for n in range(2):
                        wait("PE", f"PT {h} {n} ready", "v ready", f"bank {6 + n} drained")
                        for k in range(4):
                            i = pe.matmul(bank(6 + n)[:, k * P:(k + 1) * P], vv[:, 4 * n + k, h * HK:(h + 1) * HK],
                                          PT[:, h, n, k * P:(k + 1) * P], start=True, stop=True)
                        say("PE", i, f"bank {6 + n} filled", f"v {h} weighed")
                        wait("ACT", f"bank {6 + n} filled", "bias_v ready", "out projected")
                        affine("ACT", OT[h][:, n * BANK:(n + 1) * BANK], bank(6 + n), None, bvcol[:, h:h + 1], f"OT {h} ready",
                               f"bank {6 + n} drained")

                def output(n, b_):
                    wait("PE", "wo loaded", "OT 0 ready", "OT 1 ready", f"bank {b_} drained")
                    for k in range(2):
                        for h in range(2):
                            i = pe.matmul(bank(b_)[:, k * D:(k + 1) * D], OT[h][:, (2 * n + k) * S:(2 * n + k + 1) * S], wo[:, h, :],
                                          start=h == 0, stop=h == 1)
                    say("PE", i, f"bank {b_} filled", "out projected")
                    wait("DVE", f"bank {b_} filled", f"x {n} added")
                    say("DVE", dve.tensor_tensor(x_all[:, 2 * n:2 * n + 2, :], x_all[:, 2 * n:2 * n + 2, :],
                                                 bank(b_).rearrange("p (k d) -> p k d", k=2), ALU.add), f"x {n} added", f"bank {b_} drained")

                def pair(turn, first, last):
                    load_qk(0, turn * 2 + 1)
                    load_vo(turn)
                    if not last:
                        load_qk(1, turn * 2 + 2)
                    scores(0)
                    softmax(0)
                    if not first:
                        for n in range(4):
                            output(n, 4 + n)
                    load_o(turn)
                    project("q", 0, 1, (6, 7))
                    project("k", 0, 1, (4, 5))
                    load_bias_v(turn)
                    scores(1)
                    softmax(1)
                    for n in range(4):
                        values(n, turn, 4 + n)
                    turn_weights(0)
                    if not last:
                        project("q", 1, 0, (0, 1))
                    weigh(0)
                    turn_weights(1)
                    if not last:
                        project("k", 1, 0, (2, 3))
                    weigh(1)

                say("dma_bv", sp.dma_start(bv[:, :], ins[f"bv{j}"].partition_broadcast(P)), "bv loaded")
                say("dma_bv", sp.dma_start(bias_v[:, :], ins[f"bias_v{j}"].partition_broadcast(P)), "bv loaded")
                load_qk(1, 0)
                project("q", 1, 0, (0, 1))
                project("k", 1, 0, (2, 3))
                wait("POOL", "bv loaded")
                say("POOL", pool.tensor_tensor(bv[:, :], bv[:, :], bias_v[:, :], ALU.subtract), "bv made")
                wait("DVE", "bv made")
                pair(0, True, False)
                with p.loop(f"B{j}", NP_ - 2, but=("weights C",)) as turn:
                    pair(turn + 1, False, False)
                pair(NP_ - 1, False, True)
                for n in range(4):
                    output(n, n)

            cross_attention(1)
            p.everyone(but=("weights C",))
            for n in range(B // SB):
                x_, t = xs[n % 2], f"N{n % 2} "
                wait("POOL", t + "x normed")
                say("POOL", pool.tensor_copy(x_[:, :, :], x_all[:, n * SB:(n + 1) * SB, :]), t + "x ready")
                pool.tensor_tensor(x_all[:, n * SB:(n + 1) * SB, :], x_all[:, n * SB:(n + 1) * SB, :],
                                   row("L2_bo2").unsqueeze(1).to_broadcast([P, SB, D]), ALU.add)
                norm(t, x_, list(range(SB)), xn[n % 2], norm_st[n % 2])
                to_features(xn[n % 2], t + "xn ready", t + "xn turned", hT_all[:, :, n * T:(n + 1) * T], t + "hT_all", [],
                            col["L2_ln2_scale"], col["L2_ln2_offset"])
            p.everyone(but=("weights C",))
            cross_attention(2)

        p.everyone(but=("weights C",))
        with ExitStack() as scope:
            streams = [Stream(f"C{k} ", scope, 1) for k in range(NS)]
            sh = shared_buffers(scope, "C ")
            ms = sb("ms", [P, 2, 1, S], scope)
            mc = sb("mc", [P, 2, B, S], scope)
            mg = sb("mg", [P, 2, G, S], scope)
            say("dma_masks", sp.dma_start(ms[:, 0, 0, :], ins["mask_fc1"]), "masks loaded")
            say("dma_masks", sp.dma_start(mc[:, 0, :, :], ins["mask_ff1"].rearrange("b q k -> q b k")), "masks loaded")
            wait("DVE", "masks loaded")
            for m in (ms, mc):
                say("DVE", dve.tensor_scalar(m[:, 1, :, :], m[:, 0, :, :], 10000.0, -10000.0, ALU.mult, ALU.add), "masks made")

            with p.loop("C", NG) as turn:
                for k, s in enumerate(streams):
                    t = s.t
                    wait("POOL", t + "x stored", t + "cT used")
                    p.wait_ahead("POOL")
                    say("POOL", pool.tensor_copy(s.x[:, :, :], x_all[:, bass.ds(turn * G + k * SB, SB), :]), t + "x ready")
                    say("POOL", pool.tensor_copy(s.cT[:, :, :], ctxT_all[:, :, bass.ds(turn * G * S + k * T, T)]), t + "cT ready")
                    s.norm()
                wait("POOL", "group mask used")
                p.wait_ahead("POOL")
                say("POOL", pool.tensor_copy(mg[:, :, :, :], mc[:, :, bass.ds(turn * G, G), :]), "group mask")

                run_mlp(streams, (col["L2_ln_mlp_scale"], col["L2_ln_mlp_offset"]), w["L2_w_fc1"], col["L2_b_fc1"], ACT.Gelu,
                        w["L2_w_fc2"], "L2_b_fc2")

                def float_mask(mask, which):
                    def stage(s, b, sc, tv, per, nk, v, drained):
                        i = which(streams.index(s) * SB + b)
                        wait("DVE", "group mask")
                        say("DVE", dve.tensor_tensor(tv, sc, mask[:, 0, i:i + 1, :].to_broadcast([P, per, S]), ALU.mult),
                            f"tile {v} multiplied", *drained)
                        wait("DVE", f"tile {v} multiplied")
                        say("DVE", dve.tensor_tensor(tv, tv, mask[:, 1, i:i + 1, :].to_broadcast([P, per, S]), ALU.add),
                            f"tile {v} masked", "group mask used")
                    return stage

                def project_self(s, banks):
                    wt, bq, t = w["L3_w_qkv"], col["L3_b_qkv"], s.t
                    s.normed_features(col["L3_ln1_s"], col["L3_ln1_b"], banks)
                    s.queries(wt[:, :, 0:D], bq[:, 0:2], scale16, banks)
                    s.keys(wt[:, :, D:2 * D], bq[:, 2:4], s.hT, t + "hT ready", t + "hT used", 0, banks)
                    s.values(wt[:, :, 2 * D:3 * D], s.hT, t + "hT ready", t + "hT used", 0, banks)

                def project_cross(s, banks):
                    wt, bk, t = w["L3_w_kv"], col["L3_b_kv"], s.t
                    s.normed_features(col["L3_ln2_s"], col["L3_ln2_b"], banks)
                    s.queries(w["L3_w_q"], col["L3_b_q"], scale16, banks)
                    s.keys(wt[:, :, 0:D], bk[:, 0:2], s.cT, t + "cT ready", t + "cT used", 0, banks)
                    s.values(wt[:, :, D:2 * D], s.cT, t + "cT ready", t + "cT used", 0, banks)

                for s in streams:
                    s.norm()
                block(streams, sh, project_self, 1, float_mask(ms, lambda i: 0), col["L3_b_qkv"][:, 4:6], w["L3_w_ao"],
                      "L3_b_ao", False, False, None, None)
                block(streams, sh, project_cross, 1, float_mask(mg, lambda i: i), col["L3_b_kv"][:, 2:4], w["L3_w_co"],
                      "L3_b_co", False, False, (col["L3_ln3_s"], col["L3_ln3_b"]),
                      (w["L3_w1"], col["L3_b1"], ACT.Gelu_apprx_tanh, w["L3_w2"], "L3_b2"))
                for k, s in enumerate(streams):
                    wait("SP", s.t + "x ready")
                    say(f"dma_out{k}", sp.dma_start(out.rearrange("b s d -> s b d")[:, bass.ds(turn * G + k * SB, SB), :], s.x[:, :, :]), s.t + "x stored")
        p.everyone()
        return p.found


INPUTS = {
    "x": (B, S, D), "ctx": (B, S, D), "mask_bf1": (B * S,), "mask_ik0": (B * S,), "mask_fc1": (S, S),
    "mask_ff1": (B, S, S), "cols": (NCOL, P), "rows": (len(ROWS) * D,),
    "bv1": (H * HK,), "bv2": (H * HK,), "bias_v1": (H * HK,), "bias_v2": (H * HK,),
    "wq1": (D, H * HK), "wk1": (D, H * HK), "wv1": (D, H * HK), "wo1": (H * HK, D),
    "wq2": (D, H * HK), "wk2": (D, H * HK), "wv2": (D, H * HK), "wo2": (H * HK, D),
    "L0_q_w": (D, D), "L0_k_w": (D, D), "L0_v_w": (D, D), "L0_cproj_w": (D, D), "L0_fc_w": (D, F),
    "L0_proj_w": (F, D), "L1_q_w": (D, D), "L1_k_w": (D, D), "L1_v_w": (D, D), "L1_out_w": (D, D),
    "L1_mlp_w1": (D, F), "L1_mlp_w2": (F, D), "L2_w_fc1": (D, F), "L2_w_fc2": (F, D), "L3_w_qkv": (D, 3 * D),
    "L3_w_ao": (D, D), "L3_w_q": (D, D), "L3_w_kv": (D, 2 * D), "L3_w_co": (D, D), "L3_w1": (D, F), "L3_w2": (F, D),
}
INPUT_TYPES = {"mask_bf1": mybir.dt.uint8, "mask_ik0": mybir.dt.int32}


def declare_and_build(nc, plan):
    ins = {n: nc.dram_tensor(f"in_{n}", s, INPUT_TYPES.get(n, F32), kind="ExternalInput").ap() for n, s in INPUTS.items()}
    out = nc.dram_tensor("out_0", (B, S, D), F32, kind="ExternalOutput").ap()
    return build(nc, ins, out, plan)


def kernel(**inputs):
    import concourse.bacc as bacc
    from concourse.bass_utils import run_bass_kernel_spmd as run

    plan = declare_and_build(bacc.Bacc("TRN2", target_bir_lowering=False, num_devices=1), {})
    nc = bacc.Bacc("TRN2", target_bir_lowering=False, num_devices=1)
    declare_and_build(nc, plan)

    full = {k.replace("_xattn", ""): np.asarray(v) for k, v in inputs.items()}
    kvw, kvb = full["L1_kv_w"].reshape(D, D, 2), full["L1_kv_b"].reshape(D, 2)
    full["L1_k_w"], full["L1_v_w"], full["L1_k_b"], full["L1_v_b"] = kvw[..., 0], kvw[..., 1], kvb[:, 0], kvb[:, 1]
    arrays = {
        "x": full["x"], "ctx": full["ctx_2048"], "mask_bf1": full["mask_BxS2_bf1"].view(np.uint8).reshape(-1),
        "mask_ik0": full["mask_BxS2_ik0"].reshape(-1), "mask_fc1": full["mask_1x1xSxS2_fc1"].reshape(S, S),
        "mask_ff1": full["mask_Bx1xSxS2_ff1"].reshape(B, S, S),
        "cols": np.concatenate([full[n].reshape(-1, P) for n, _ in COLS]),
        "rows": np.concatenate([full[n].reshape(-1) for n in ROWS]),
    }
    for n in INPUTS:
        if n not in arrays:
            src = full[n] if n in full else full["L2_" + n]
            arrays[n] = src.reshape(INPUTS[n])
    arrays = {f"in_{n}": np.ascontiguousarray(a) for n, a in arrays.items()}
    r = run(nc, [arrays], core_ids=[0])
    return r.results[0]["out_0"]
```

```python
import numpy as np

import concourse.bass as bass
from concourse import mybir
from concourse.alu_op_type import AluOpType as ALU
from contextlib import ExitStack, contextmanager

F32 = mybir.dt.float32
F32R = mybir.dt.float32r
ACT = mybir.ActivationFunctionType
AX = mybir.AxisListType

P = 128
B, S, D = 8, 128, 256
H, HD = 16, 16
HK = 128
F = 1024
G = 4
NG = B // G
NS = 2
SB = G // NS
T = SB * S
C = D // P
FC = F // P
HC = P // HD
BANK = 512
BIG = 3.4028234663852886e38

COLS = [("L0_ln1_w", 2), ("L0_ln1_b", 2), ("L0_q_b", 2), ("L0_k_b", 2), ("L0_v_b", 2), ("L0_ln2_w", 2),
        ("L0_ln2_b", 2), ("L0_fc_b", 8), ("L1_q_b", 2), ("L1_k_b", 2), ("L1_v_b", 2), ("L1_postnorm_w", 2),
        ("L1_mlp_b1", 8), ("L2_ln1_scale", 2), ("L2_ln1_offset", 2), ("L2_bq1", 16), ("L2_bk1", 16),
        ("L2_bias_k1", 16), ("L2_bias_v1", 16), ("L2_ln2_scale", 2), ("L2_ln2_offset", 2), ("L2_bq2", 16),
        ("L2_bk2", 16), ("L2_bias_k2", 16), ("L2_bias_v2", 16), ("L2_ln_mlp_scale", 2),
        ("L2_ln_mlp_offset", 2), ("L2_b_fc1", 8), ("L3_ln1_s", 2), ("L3_ln1_b", 2), ("L3_b_qkv", 6),
        ("L3_ln2_s", 2), ("L3_ln2_b", 2), ("L3_b_q", 2), ("L3_b_kv", 4), ("L3_ln3_s", 2), ("L3_ln3_b", 2),
        ("L3_b1", 8)]
NCOL = sum(n for _, n in COLS)
ROWS = ["L0_cproj_b", "L0_proj_b", "L1_out_b", "L1_mlp_b2", "L2_bo1", "L2_bo2", "L2_b_fc2", "L3_b_ao", "L3_b_co",
        "L3_b2"]

WEIGHTS_A = [("L0_q_w", D, D), ("L0_k_w", D, D), ("L0_v_w", D, D), ("L0_cproj_w", D, D), ("L0_fc_w", D, F), ("L0_proj_w", F, D),
             ("L1_q_w", D, D), ("L1_k_w", D, D), ("L1_v_w", D, D), ("L1_out_w", D, D), ("L1_mlp_w1", D, F), ("L1_mlp_w2", F, D)]
WEIGHTS_C = [("L2_w_fc1", D, F), ("L2_w_fc2", F, D), ("L3_w_qkv", D, 3 * D), ("L3_w_ao", D, D), ("L3_w_q", D, D),
             ("L3_w_kv", D, 2 * D), ("L3_w_co", D, D), ("L3_w1", D, F), ("L3_w2", F, D)]
WEIGHT_COLS = sum(k // P * n for _, k, n in WEIGHTS_A)
assert WEIGHT_COLS == sum(k // P * n for _, k, n in WEIGHTS_C)


class Counter:

    def __init__(self, sem, base):
        self.sem, self.base, self.here = sem, base, 0


class Program:
    def __init__(self, nc, ctx, plan):
        self.nc, self.ctx, self.plan, self.found = nc, ctx, plan, {"seed": {}, "events": set()}
        self.engines = {"PE": nc.tensor, "ACT": nc.scalar, "DVE": nc.vector, "POOL": nc.gpsimd, "SP": nc.sync}
        self.counters, self.idle = {}, {}
        self.said = {}
        self.reached = {}
        self.turn, self.step = None, {}
        for name in ["PE", "ACT", "DVE", "POOL"] + list(plan.get("seed", {})):
            self.counter(name)

    def counter(self, name):
        if name not in self.counters:
            sem = self.ctx.enter_context(self.nc.semaphore(f"s_{name}"))
            seed = self.plan.get("seed", {}).get(name, 0)
            if seed:
                self.nc.sync.sem_inc(sem, seed)
            self.counters[name] = Counter(sem, seed)
        return self.counters[name]

    def say(self, name, instr, *events):
        c = self.counter(name)
        by = 1 if name in self.engines else 16
        instr.then_inc(c.sem, by)
        c.here += by
        for event in events:
            self.said[event] = (name, c.here, 0)
            self.found["events"].add(event)
        return instr

    def wait(self, engine, *events):
        most = {}
        for event in events:
            if event not in self.said:
                assert self.turn is None or event not in self.plan.get("events", ()), event
                continue
            name, value, back = self.said[event]
            value -= back * self.step.get(name, 0)
            most[name] = max(most.get(name, value), value)
        for name, value in most.items():
            if self.reached.get((engine, name), value - 1) >= value:
                continue
            self.reached[engine, name] = value
            c = self.counters[name]
            at = c.base + value
            if self.turn is not None and self.step.get(name, 0):
                at = self.turn * self.step[name] + at
            self.engines[engine].wait_ge(c.sem, at)
            if engine == "SP":
                self.wait_ahead(engine)

    def wait_ahead(self, engine):
        if self.turn is None:
            return
        if engine not in self.idle:
            self.idle[engine] = self.ctx.enter_context(self.nc.semaphore(f"idle_{engine}"))
        self.engines[engine].sem_inc(self.idle[engine], 1)

    def everyone(self, but=()):
        for name, c in self.counters.items():
            if name in but or not c.here:
                continue
            for engine in self.engines:
                if self.reached.get((engine, name), c.here - 1) < c.here:
                    self.engines[engine].wait_ge(c.sem, c.base + c.here)
        keep = {n for n in self.counters if n in but}
        self.said = {e: (n, v, b) for e, (n, v, b) in self.said.items() if n in keep}
        for n, c in self.counters.items():
            if n not in keep:
                c.base, c.here = c.base + c.here, 0
        self.reached = {}

    @contextmanager
    def loop(self, name, turns, but=()):
        self.everyone(but)
        plan = self.plan.get(name, {"step": {}, "said": {}})
        self.step = plan["step"]
        for event, (n, v) in plan["said"].items():
            self.said[event] = (n, v, 1)
        with self.nc.Fori(0, turns) as turn:
            self.turn = turn
            yield turn
        step = {n: c.here for n, c in self.counters.items() if c.here and n not in but}
        assert not self.plan or plan["step"] == step, (name, plan["step"], step)
        self.found[name] = {"step": step, "said": {e: (n, v) for e, (n, v, b) in self.said.items() if not b and n not in but}}
        for n, v in step.items():
            self.found["seed"][n] = max(self.found["seed"].get(n, 0), v)
            self.counters[n].base += (turns - 1) * v
        self.turn, self.step, self.reached = None, {}, {}
        self.said = {e: (n, v, 0) for e, (n, v, b) in self.said.items() if not b}


def staged(n, stages, at=None):
    for t in range(n + max(lag for lag, _ in stages)):
        if at and t in at:
            at[t]()
        for lag, stage in stages:
            if 0 <= t - lag < n:
                stage(t - lag)


def build(nc, ins, out, plan):
    with ExitStack() as ctx:
        p = Program(nc, ctx, plan)
        say, wait = p.say, p.wait
        pe, act, dve, pool, sp = nc.tensor, nc.scalar, nc.vector, nc.gpsimd, nc.sync

        def sb(name, shape, where=ctx, dtype=F32):
            return where.enter_context(nc.sbuf_tensor(name, shape, dtype))

        psum = ctx.enter_context(nc.psum_tensor("psum", [P, 8, BANK], F32))

        def bank(k):
            return psum[:, k, :]

        ident = sb("ident", [P, P])
        of_head = sb("of_head", [P, HC])
        cols = sb("cols", [P, NCOL])
        col_rows = sb("col_rows", [P, 2, P])
        rows = sb("rows", [P, len(ROWS), D])
        half = sb("half", [P, G])
        weights = sb("weights", [P, WEIGHT_COLS])
        x_all = sb("x_all", [P, B, D])
        ctxT_all = sb("ctxT_all", [P, C, B * S])
        hT_all = sb("hT_all", [P, C, B * S])
        ms = sb("ms", [P, 2, 1, S])
        mc = hT_all[:, :, :].rearrange("p n (b s) -> p n b s", s=S)

        col, at = {}, 0
        for name, n in COLS:
            col[name] = cols[:, at:at + n]
            at += n

        def row(name):
            return rows[:, ROWS.index(name), :]

        for k in range(2):
            n = min(P, NCOL - k * P)
            say("dma_setup", sp.dma_start(col_rows[0:n, k, :], ins["cols"][k * P:k * P + n, :]), "cols loaded")

        w = {}

        def place_weights(table):
            at = 0
            for name, k, n in table:
                w[name] = weights[:, at:at + k // P * n].rearrange("p (c n) -> p c n", n=n)
                at += k // P * n

        pool.memset(half[:, :], -0.5)
        say("POOL", pool.memset(ident[:, :], 0.0), "ident cleared")
        say("POOL", pool.memset(of_head[:, :], 1.0), "of_head filled")
        wait("POOL", "ident cleared")
        say("POOL", pool.affine_select(out=ident[:, :], in_=ident[:, :], compare_op=ALU.not_equal, fill=1.0,
                                       base=0, pattern=[[-1, P]], channel_multiplier=1), "ident made")
        wait("POOL", "of_head filled")
        say("POOL", pool.affine_select(out=of_head[:, :], in_=of_head[:, :], compare_op=ALU.is_ge, fill=0.0, base=0,
                                       pattern=[[-HD, HC]], channel_multiplier=1), "of_head cut below")
        wait("POOL", "of_head cut below")
        say("POOL", pool.affine_select(out=of_head[:, :], in_=of_head[:, :], compare_op=ALU.is_ge, fill=0.0, base=HD - 1,
                                       pattern=[[HD, HC]], channel_multiplier=-1), "of_head made")
        wait("PE", "ident made")
        wait("PE", "cols loaded")
        for k in range(2):
            n = min(P, NCOL - k * P)
            say("PE", pe.transpose(bank(1)[:, k * P:k * P + n], col_rows[0:n, k, :], ident[0:n, 0:n]), "cols turned")
        wait("DVE", "cols turned")
        say("DVE", dve.tensor_copy(cols[:, :], bank(1)[:, 0:NCOL]), "cols made", "bank 1 drained")
        wait("DVE", "cols made")
        scale16 = float(1.0 / np.sqrt(np.float32(HD)))
        scaleK = float(1.0 / np.sqrt(np.float32(HK)))
        scale_of = {"L0_q_b": scale16, "L1_q_b": 1.0 / HD, "L3_b_q": scale16, "L2_bq1": scaleK, "L2_bq2": scaleK}
        for name, scale in scale_of.items():
            dve.tensor_scalar(col[name], col[name], scale, None, ALU.mult)
        dve.tensor_scalar(col["L3_b_qkv"][:, 0:C], col["L3_b_qkv"][:, 0:C], scale16, None, ALU.mult)
        for j in "12":
            say("DVE", dve.tensor_tensor(col["L2_bk" + j], col["L2_bk" + j], col["L2_bias_k" + j], ALU.subtract), "cols made")

        lin = {"bank": 0, "engine": 0}

        def next_bank(of):
            lin["bank"] += 1
            return of[lin["bank"] % len(of)]

        def next_engine():
            lin["engine"] += 1
            return ("ACT", "DVE")[lin["engine"] % 2]

        ALL = tuple(range(8))
        UPPER = (4, 5, 6, 7)
        FEED = {0: 1, 2: 2}
        LOWER = (0, 1, 2, 3)

        def affine(e, dst, src, scale, bias, *events):
            if e == "ACT":
                i = act.activation(dst, src, ACT.Identity, bias=0.0 if bias is None else bias,
                                   scale=1.0 if scale is None else scale)
            elif bias is None:
                i = dve.tensor_scalar(dst, src, 1.0 if scale is None else scale, None, ALU.mult)
            elif scale is None:
                i = dve.tensor_scalar(dst, src, bias, None, ALU.add)
            else:
                i = dve.tensor_scalar(dst, src, scale, bias, ALU.mult, ALU.add)
            say(e, i, *events)

        def norm(tag, x, batches, xn, st, rms=False):
            eps = 1e-6 if rms else 1e-5
            lo, hi = batches[0], batches[-1] + 1
            mean = st["mv"][:, lo:hi, 0]
            var = st["mv"][:, lo:hi, 1]
            wait("DVE", tag + "x ready")
            for b in batches:
                say("DVE", dve.bn_stats(st["bn"][:, 6 * b:6 * b + 6], x[:, b, :]), tag + "stats")
            wait("DVE", tag + "stats", tag + "ve read")
            p.wait_ahead("DVE")
            for b in batches:
                say("DVE", dve.bn_aggr(st["mv"][:, b, :], st["bn"][:, 6 * b:6 * b + 6]), tag + "moments")
            wait("DVE", tag + "moments")
            if rms:
                say("DVE", dve.tensor_tensor(st["ve"][:, lo:hi], mean, mean, ALU.mult), tag + "mean squared")
                wait("DVE", tag + "mean squared")
                say("DVE", dve.scalar_tensor_tensor(out=st["ve"][:, lo:hi], in0=st["ve"][:, lo:hi], scalar=eps, in1=var,
                                                    op0=ALU.add, op1=ALU.add), tag + "ve")
            else:
                say("DVE", dve.tensor_scalar(st["ve"][:, lo:hi], var, eps, None, ALU.add), tag + "ve")
            wait("POOL", tag + "ve")
            say("POOL", pool.tensor_tensor(st["rstd"][:, lo:hi], st["ve"][:, lo:hi], half[:, 0:hi - lo], ALU.pow),
                tag + "rstd", tag + "ve read")
            wait("DVE", tag + "rstd", tag + "xn turned")
            for b in batches:
                if rms:
                    i = dve.tensor_scalar(xn[:, b, :], x[:, b, :], st["rstd"][:, b:b + 1], None, ALU.mult)
                else:
                    i = dve.tensor_scalar(xn[:, b, :], x[:, b, :], st["mv"][:, b, 0:1], st["rstd"][:, b:b + 1],
                                          ALU.subtract, ALU.mult)
                say("DVE", i, tag + "xn ready", tag + "x normed")

        def to_features(src, ready, turned, dst, dst_ready, dst_free, scale=None, bias=None, banks=ALL, engine=None):
            k = next_bank(banks)
            wait("PE", ready, f"bank {k} drained")
            for c in range(C):
                for b in range(SB):
                    i = pe.transpose(bank(k)[:, (c * SB + b) * P:(c * SB + b + 1) * P], src[:, b, c * P:(c + 1) * P], ident[:, :])
            say("PE", i, f"bank {k} filled", turned)
            e = engine or next_engine()
            wait(e, f"bank {k} filled", *dst_free)
            for c in range(C):
                affine(e, dst[:, c, :], bank(k)[:, c * T:(c + 1) * T], None if scale is None else scale[:, c:c + 1],
                       None if bias is None else bias[:, c:c + 1], dst_ready, f"bank {k} drained")

        def linear_features(wt, src, ready, used, outs, drain, banks=ALL):
            for m in outs[::2]:
                k = next_bank(banks)
                wait("PE", ready, f"bank {k} drained")
                for n in range(2):
                    for c in range(C):
                        i = pe.matmul(bank(k)[:, n * T:(n + 1) * T], wt[:, c, (m + n) * P:(m + n + 1) * P], src[:, c, :],
                                      start=c == 0, stop=c == C - 1)
                say("PE", i, f"bank {k} filled", used)
                drain(m, k)

        def linear_tokens(wt, src, ready, used, banks=ALL):
            k = next_bank(banks)
            wait("PE", ready, f"bank {k} drained")
            for b in range(SB):
                for c in range(C):
                    i = pe.matmul(bank(k)[:, b * D:(b + 1) * D], src[:, c, b * P:(b + 1) * P], wt[:, c, :],
                                  start=c == 0, stop=c == C - 1)
            say("PE", i, f"bank {k} filled", used)
            return k

        class Stream:

            def __init__(self, t, where, n_src):
                def b(name, shape):
                    return sb(t + name, shape, where)
                self.t, self.n_src = t, n_src
                self.x, self.xb, self.xn = (b(n, [P, SB, D]) for n in ("x", "xb", "xn"))
                self.hT, self.cT, self.qT = (b(n, [P, C, T]) for n in ("hT", "cT", "qT"))
                self.kT = b("kT", [P, C, n_src, T])
                self.qm = b("qm", [P, C, HC, T])
                self.vaug = b("vaug", [P, n_src, SB, H, HD + 1])
                self.OT = b("OT", [P, SB, C, P])
                self.aT = self.qm[:, 0, :, :]
                self.on = b("on", [P, D])
                self.rec = b("rec", [P, H])
                self.st = {"bn": b("bn", [P, 6 * SB]), "mv": b("mv", [P, SB, 2]), "ve": b("ve", [P, SB]), "rstd": b("rstd", [P, SB])}
                say("POOL", pool.memset(self.vaug[:, :, :, :, HD:HD + 1], 1.0), "ones set")

            def fetch(self, turn, k):
                t = self.t
                wait("ACT", t + "x stored", t + "x copied", t + "x normed", t + "x turned", t + "cT used")
                p.wait_ahead("ACT")
                say("ACT", act.copy(self.x[:, :, :], x_all[:, bass.ds(turn * G + k * SB, SB), :]), t + "x ready")
                say("ACT", act.copy(self.cT[:, :, :], ctxT_all[:, :, bass.ds(turn * G * S + k * T, T)]), t + "cT ready")

            def norm(self, x=None, batches=range(SB), rms=False):
                norm(self.t, self.x if x is None else x, list(batches), self.xn, self.st, rms)

            def normed_features(self, scale, bias, banks=ALL):
                t = self.t
                to_features(self.xn, t + "xn ready", t + "xn turned", self.hT, t + "hT ready", [t + "hT used"], scale, bias, banks)

            def residual(self, name):
                t = self.t
                wait("POOL", t + "x ready", t + "xb used", t + "x normed")
                say("POOL", pool.tensor_tensor(self.xb[:, :, :], self.x[:, :, :],
                                               row(name).unsqueeze(1).to_broadcast([P, SB, D]), ALU.add), t + "xb ready", t + "x copied")

            def queries(self, wt, bias, scale, banks=ALL):
                t = self.t

                def drain(m, k):
                    wait("DVE", f"bank {k} filled", t + "qT spread 0", t + "qT spread 1")
                    for n in range(2):
                        affine("DVE", self.qT[:, n, :], bank(k)[:, n * T:(n + 1) * T], scale, bias[:, n:n + 1],
                               t + "qT ready", f"bank {k} drained")
                    self.spread()
                linear_features(wt, self.hT, t + "hT ready", t + "hT used", range(C), drain, banks)

            def spread(self):
                t = self.t
                wait("DVE", t + "qT ready", t + "qm used", t + "aT used")
                for j in range(HC):
                    affine("DVE", self.qm[:, 0, j, :], self.qT[:, 0, :], of_head[:, j:j + 1], None, t + "qm 0 ready", t + "qT spread 0")
                wait("POOL", t + "qT ready", t + "qm used")
                say("POOL", pool.tensor_tensor(self.qm[:, 1, :, :], self.qT[:, 1:2, :].to_broadcast([P, HC, T]),
                                               of_head[:, :].unsqueeze(2).to_broadcast([P, HC, T]), ALU.mult),
                    t + "qm 1 ready", t + "qT spread 1")

            def keys(self, wt, bias, src, ready, used, s, banks=ALL):
                t = self.t

                def drain(m, k):
                    wait("ACT", f"bank {k} filled", t + "kT used")
                    for n in range(2):
                        affine("ACT", self.kT[:, n, s, :], bank(k)[:, n * T:(n + 1) * T], None, bias[:, n:n + 1], t + f"kT {s} ready",
                               f"bank {k} drained")
                linear_features(wt, src, ready, used, range(C), drain, banks)

            def values(self, wt, src, ready, used, s, banks=ALL):
                t = self.t
                k = linear_tokens(wt, src, ready, used, banks)
                wait("ACT", f"bank {k} filled", t + "vaug used")
                affine("ACT", self.vaug[:, s, :, :, 0:HD].rearrange("p b h d -> p (b h) d"),
                       bank(k).rearrange("p (g d) -> p g d", d=HD), None, None, t + "vaug ready", f"bank {k} drained")

            def mlp_up(self, w1, b1, func, outs=range(FC), banks=ALL):
                t = self.t

                def drain(m, k):
                    wait("ACT", f"bank {k} filled", t + "aT used", t + "qm used")
                    for n in range(2):
                        say("ACT", act.activation(self.aT[:, m + n, :], bank(k)[:, n * T:(n + 1) * T], func,
                                                  bias=b1[:, m + n:m + n + 1]), t + "aT ready", f"bank {k} drained")
                linear_features(w1, self.hT, t + "hT ready", t + "hT used", outs, drain, banks)

            def mlp_down(self, w2):
                t = self.t
                k = next_bank(ALL)
                wait("PE", t + "aT ready", f"bank {k} drained")
                for b in range(SB):
                    for c in range(FC):
                        i = pe.matmul(bank(k)[:, b * D:(b + 1) * D], self.aT[:, c, b * P:(b + 1) * P], w2[:, c, :],
                                      start=c == 0, stop=c == FC - 1)
                say("PE", i, f"bank {k} filled", t + "aT used")
                wait("DVE", f"bank {k} filled", t + "xb ready", t + "x copied", t + "x turned", t + "x stored")
                say("DVE", dve.tensor_tensor(self.x[:, :, :], bank(k).rearrange("p (b d) -> p b d", b=SB), self.xb[:, :, :],
                                             ALU.add), t + "x ready", t + "xb used", f"bank {k} drained")

        def attention(streams, sh, n_src, mask_stage, v_bias, w_out, into_xb, after, at):
            per = 8 // n_src
            nk = n_src * S
            n_batch = H // per
            units = [(s, b, k * per // HC, k * per % HC, k % 2) for s in streams for b in range(SB) for k in range(n_batch)]

            def drained(r):
                return f"bank {2 * r} drained", f"bank {2 * r + 1} drained"

            def scores(u):
                s, b, c, h0, r = units[u]
                wait("PE", s.t + f"qm {c} ready", *(s.t + f"kT {n} ready" for n in range(n_src)), *drained(r))
                both = psum[:, 2 * r:2 * r + 2, :].rearrange("p g k -> p (g k)")
                for n in range(per):
                    i = pe.matmul(both[:, n * nk:(n + 1) * nk], s.qm[:, c, h0 + n, b * S:(b + 1) * S],
                                  s.kT[:, c, 0:n_src, b * S:(b + 1) * S], start=True, stop=True)
                say("PE", i, f"banks {r} scored", s.t + "qm used", s.t + "kT used")

            def softmax(u):
                s, b, _, _, r = units[u]
                v = u % len(sh["tiles"])
                tile = sh["tiles"][v]
                tv = tile[:, :].rearrange("p (h k) -> p h k", k=nk)
                sc = psum[:, 2 * r:2 * r + 2, :].rearrange("p g (h k) -> p (g h) k", k=nk)
                wait("DVE", f"banks {r} scored", f"tile {v} turned")
                mask_stage(s, b, sc, tv, per, nk, v, drained(r))
                mx = sh["max"][:, u % 2, 0:per]
                wait("DVE", f"tile {v} masked", f"max {u % 2} used")
                say("DVE", dve.tensor_reduce(mx, tv, AX.X, ALU.max), f"max {u % 2}")
                wait("POOL", f"max {u % 2}")
                say("POOL", pool.tensor_tensor(tv, tv, mx.unsqueeze(2).to_broadcast([P, per, nk]), ALU.subtract),
                    f"tile {v} shifted", f"max {u % 2} used")
                wait("ACT", f"tile {v} shifted")
                say("ACT", act.activation(tile[:, :], tile[:, :], ACT.Exp), f"tile {v} exp")

            def turn(u):
                v = u % len(sh["tiles"])
                for n in range(2):
                    wait("PE", f"tile {v} exp", f"bank {4 + n} drained")
                    for q in range(4):
                        i = pe.transpose(bank(4 + n)[:, q * P:(q + 1) * P], sh["tiles"][v][:, (4 * n + q) * P:(4 * n + q + 1) * P], ident[:, :])
                    say("PE", i, f"bank {4 + n} filled", f"tile {v} turned")
                    wait("ACT", f"bank {4 + n} filled", f"PT {u % 2} used")
                    say("ACT", act.copy(sh["PT"][:, u % 2, n, :], bank(4 + n)), f"PT {u % 2} {n} ready", f"bank {4 + n} drained")

            def weigh(u):
                s, b, c, h0, _ = units[u]
                if u % n_batch == 0:
                    wait("PE", "bank 6 drained")
                for n in range(per):
                    h = HC * c + h0 + n
                    for src in range(n_src):
                        q = n * n_src + src
                        wait("PE", f"PT {u % 2} {q // 4} ready", s.t + "vaug ready")
                        i = pe.matmul(bank(6)[:, h * 17:(h + 1) * 17], sh["PT"][:, u % 2, q // 4, (q % 4) * P:(q % 4 + 1) * P],
                                      s.vaug[:, src, b, h, :], start=src == 0, stop=src == n_src - 1)
                say("PE", i, "bank 6 filled", f"PT {u % 2} used", s.t + "vaug used")

            def last(stage):
                return lambda u: stage(*units[u][0:2]) if u % n_batch == n_batch - 1 else None

            def divide(s, b):
                t = s.t
                ov = bank(6)[:, 0:H * 17].rearrange("p (h d) -> p h d", d=17)
                wait("DVE", "bank 6 filled", t + "on turned")
                say("DVE", dve.reciprocal(s.rec[:, :].unsqueeze(2), ov[:, :, 16:17]), t + "rec")
                wait("DVE", t + "rec")
                say("DVE", dve.tensor_tensor(s.on[:, :].rearrange("p (h d) -> p h d", d=HD), ov[:, :, 0:HD],
                                             s.rec[:, :].unsqueeze(2).to_broadcast([P, H, HD]), ALU.mult), t + "on ready", "bank 6 drained")

            def features(s, b):
                t = s.t
                wait("PE", t + "on ready", "bank 7 drained")
                for c in range(C):
                    i = pe.transpose(bank(7)[:, c * P:(c + 1) * P], s.on[:, c * P:(c + 1) * P], ident[:, :])
                say("PE", i, "bank 7 filled", t + "on turned")
                wait("DVE", "bank 7 filled", t + f"OT {b} used")
                for c in range(C):
                    affine("DVE", s.OT[:, b, c, :], bank(7)[:, c * P:(c + 1) * P], None, v_bias[:, c:c + 1], t + f"OT {b} ready", "bank 7 drained")

            def project(s, b):
                t = s.t
                wait("PE", t + f"OT {b} ready", "bank 7 drained")
                for c in range(C):
                    i = pe.matmul(bank(7)[:, 0:D], s.OT[:, b, c, :], w_out[:, c, :], start=c == 0, stop=c == C - 1)
                say("PE", i, "bank 7 filled", t + f"OT {b} used")
                wait("DVE", "bank 7 filled", t + "xb ready", *([] if into_xb else [t + "x copied", t + "x turned"]))
                say("DVE", dve.tensor_tensor((s.xb if into_xb else s.x)[:, b, :], bank(7)[:, 0:D], s.xb[:, b, :], ALU.add),
                    t + "x ready", t + "xb used", "bank 7 drained")
                after(s, b)

            staged(len(units), [(0, scores), (2, turn), (0, softmax), (3, weigh), (3, last(divide)), (4, last(features)),
                                (5, last(project))], at)

        def shared_buffers(where, t):
            return {"tiles": [sb(f"{t}tile{k}", [P, 2 * BANK], where) for k in range(3)],
                    "PT": sb(t + "PT", [P, 2, 2, BANK], where), "max": sb(t + "max", [P, 2, 8], where)}

        def block(streams, sh, project_in, n_src, mask_stage, v_bias, w_out, row_out, into_xb, rms, meanwhile, started=False):
            for s in streams[1:] if started else streams:
                s.residual(row_out)
            if not started:
                list(project_in(streams[0], ALL))
            n_units = NS * SB * 2 * n_src
            second = project_in(streams[1], UPPER)
            at = {k: lambda n=n: [next(second, None) for _ in range(n)] for k, n in FEED.items()}
            at.update({n_units + (2 if n_src == 1 else 0) + k: f for k, f in enumerate(meanwhile)})
            attention(streams, sh, n_src, mask_stage, v_bias, w_out, into_xb,
                      lambda s, b: s.norm(s.xb if into_xb else s.x, [b], rms), at)

        class MLP:

            def __init__(self, streams, scale_bias, w1, b1, func, w2, row_out, after=lambda s: None, loaded=()):
                self.streams, self.scale_bias, self.up, self.w2 = streams, scale_bias, (w1, b1, func), w2
                self.row_out, self.after, self.loaded = row_out, after, loaded

            def begin(self, banks=LOWER):
                wait("PE", *self.loaded)
                first = self.streams[0]
                first.residual(self.row_out)
                first.normed_features(*self.scale_bias, banks)

            def meanwhile(self):
                first = self.streams[0]
                return [self.begin] + [lambda outs=outs: first.mlp_up(*self.up, outs, LOWER) for outs in (range(FC // 2), range(FC // 2, FC))]

            def rest(self):
                first, second = self.streams
                second.residual(self.row_out)
                second.normed_features(*self.scale_bias)
                first.mlp_down(self.w2)
                self.after(first)
                second.mlp_up(*self.up)
                second.mlp_down(self.w2)
                self.after(second)

            def all(self):
                self.begin(ALL)
                self.streams[0].mlp_up(*self.up)
                self.rest()

        raw = {f"{n}{k}": sb(f"raw {n}{k}", [P, C, HK]) for n in "qk" for k in range(2)}
        raw["v"], raw["o"] = sb("raw v", [P, C, 2 * HK]), sb("raw o", [P, 2, D])

        def load_qk_weights(j, k, head):
            for n in "qk":
                wait("SP", f"w{n}{k} cut")
                say(f"dma_w{n}{k}", sp.dma_start(raw[f"{n}{k}"][:, :, :], ins[f"w{n}{j}"].rearrange("(c p) n -> p c n", p=P)[:, :, bass.ds(head * HK, HK)]),
                    f"w{n}{k} loaded")

        with ExitStack() as scope:
            streams = [Stream(f"A{k} ", scope, 2) for k in range(NS)]
            sh = shared_buffers(scope, "A ")
            m0 = sb("m0", [P, B, S], scope)
            m1 = sb("m1", [P, B, 2, S], scope)
            m0_raw = sh["tiles"][0][:, 0:B * S // 4].bitcast(mybir.dt.uint8)
            m1_raw = sh["tiles"][1][:, :].bitcast(mybir.dt.int32)
            place_weights(WEIGHTS_A)
            ctx_raw = hT_all[:, :, :].rearrange("p c t -> p (c t)").rearrange("p (b d) -> p b d", b=B)
            say("dma_ctx", sp.dma_start(ctx_raw, ins["ctx"].rearrange("b s d -> s b d")), "ctx loaded")
            say("dma_x", sp.dma_start(x_all[:, :, :], ins["x"].rearrange("b s d -> s b d")), "x loaded")
            say("dma_setup2", sp.dma_start(m0_raw, ins["mask_bf1"].partition_broadcast(P)), "key masks loaded")
            say("dma_setup2", sp.dma_start(m1_raw, ins["mask_ik0"].partition_broadcast(P)), "key masks loaded")
            late, done = ("L0 attention weights", "L0 MLP weights", "L1 weights"), 0
            for counter, n in zip(late, (4, 6, len(WEIGHTS_A))):
                until = sum(k // P * cols_ for _, k, cols_ in WEIGHTS_A[:n])
                say(counter, sp.dma_start(weights[:, done:until], ins["weights_a"][:, done:until]), counter)
                done = until
                if n == 4:
                    say("rows", sp.dma_start(rows[:, :, :].rearrange("p a b -> p (a b)"), ins["rows"].partition_broadcast(P)), "rows loaded")
            for n in range(B // SB):
                to_features(ctx_raw[:, n * SB:(n + 1) * SB, :], "ctx loaded", "ctx turned", ctxT_all[:, :, n * T:(n + 1) * T], "ctxT ready", [])
            say("POOL", pool.memset(m1[:, :, 1, :], 0.0), "m1 cleared")
            wait("DVE", "key masks loaded")
            dve.tensor_scalar(m0[:, :, :].rearrange("p b s -> p (b s)"), m0_raw, 0.0, -BIG, ALU.is_equal, ALU.mult)
            say("DVE", dve.tensor_scalar(m1[:, :, 0, :], m1_raw.rearrange("p (b s) -> p b s", b=B), 0.0, -BIG, ALU.is_equal,
                                         ALU.mult), "masks made")

            load_qk_weights(1, 1, 0)
            with p.loop("A", NG, but=late + ("rows", "dma_wq1", "dma_wk1")) as turn:
                for k, s in enumerate(streams):
                    s.fetch(turn, k)
                    s.norm()

                wait("POOL", "rows loaded")

                def key_mask(mask, n):
                    def stage(s, b, sc, tv, per, nk, v, drained):
                        i = turn * G + streams.index(s) * SB + b
                        mb = mask[:, bass.ds(i, 1), :].to_broadcast([P, per, nk])
                        say("DVE", dve.tensor_tensor(tv, sc, mb, ALU.add), f"tile {v} masked", *drained)
                    return stage

                def project_in0(s, banks):
                    t = s.t
                    wait("PE", "L0 attention weights")
                    s.normed_features(col["L0_ln1_w"], col["L0_ln1_b"], banks)
                    yield
                    s.queries(w["L0_q_w"], col["L0_q_b"], scale16, banks)
                    yield
                    s.keys(w["L0_k_w"], col["L0_k_b"], s.cT, t + "cT ready", t + "cT used", 0, banks)
                    s.values(w["L0_v_w"], s.cT, t + "cT ready", t + "cT used", 0, banks)

                mlp = MLP(streams, (col["L0_ln2_w"], col["L0_ln2_b"]), w["L0_fc_w"], col["L0_fc_b"], ACT.Gelu_apprx_tanh,
                          w["L0_proj_w"], "L0_proj_b", loaded=("L0 MLP weights",))
                block(streams, sh, project_in0, 1, key_mask(m0, 1), col["L0_v_b"], w["L0_cproj_w"], "L0_cproj_b", False, False,
                      mlp.meanwhile())
                mlp.rest()

                def project_in1(s, banks):
                    t = s.t
                    wait("PE", "L1 weights")
                    to_features(s.x, t + "x ready", t + "x turned", s.hT, t + "hT ready", [t + "hT used"], banks=banks)
                    yield
                    s.queries(w["L1_q_w"], col["L1_q_b"], 1.0 / HD, banks)
                    yield
                    for n, (src, name) in enumerate(((s.cT, "cT"), (s.hT, "hT"))):
                        s.keys(w["L1_k_w"], col["L1_k_b"], src, f"{t}{name} ready", f"{t}{name} used", n, banks)
                        s.values(w["L1_v_w"], src, f"{t}{name} ready", f"{t}{name} used", n, banks)

                mlp = MLP(streams, (col["L1_postnorm_w"], None), w["L1_mlp_w1"], col["L1_mlp_b1"], ACT.Gelu_apprx_tanh,
                          w["L1_mlp_w2"], "L1_mlp_b2", lambda s: s.norm())
                block(streams, sh, project_in1, 2, key_mask(m1[:, :, :, :].rearrange("p b n s -> p b (n s)"), 2), col["L1_v_b"],
                      w["L1_out_w"], "L1_out_b", True, True, mlp.meanwhile())
                mlp.rest()
                for k, s in enumerate(streams):
                    t = s.t
                    to_features(s.xn, t + "xn ready", t + "xn turned", hT_all[:, :, bass.ds(turn * G * S + k * T, T)], t + "hT_all", [],
                                col["L2_ln1_scale"], col["L2_ln1_offset"], engine="DVE")
                    wait("POOL", t + "x ready")
                    p.wait_ahead("POOL")
                    say("POOL", pool.tensor_tensor(x_all[:, bass.ds(turn * G + k * SB, SB), :], s.x[:, :, :],
                                                   row("L2_bo1").unsqueeze(1).to_broadcast([P, SB, D]), ALU.add), t + "x stored")

        p.everyone()
        place_weights(WEIGHTS_C)

        with ExitStack() as scope:
            NP_ = H // 2
            PIECE = WEIGHT_COLS // (NP_ - 2)

            def b2(name, shape):
                return sb(f"B {name}", shape, scope)

            def parts(name, shape):
                return [sb(f"B {name} {part}", shape, scope, F32R) for part in ("hi", "lo")]

            PASSES = ((0, 0), (0, 1), (1, 0))
            cut = {n: parts(n, [P, 2, t.shape[-1]]) for n, t in raw.items()}
            hT, cT = parts("hT", [P, C, B * S]), parts("cT", [P, C, B * S])
            qT = [b2(f"qT{k}", [P, B * S]) for k in range(2)]
            kT = [b2(f"kT{k}", [P, B * S]) for k in range(2)]
            vv = b2("v", [P, B, 2 * HK])
            tiles = [b2(f"tile{k}", [P, B * S]) for k in range(2)]
            PT = b2("PT", [P, 2, 2, BANK])
            OT = [parts(f"OT{k}", [P, B * S]) for k in range(2)]
            st2 = {n: b2(n, [P, 2, B]) for n in ("max", "own", "sum", "rec")}
            bv = b2("bv", [P, H * HK])
            bcol = b2("bcol", [P, 2, 2])
            bvcol = b2("bvcol", [P, 2])
            norm_st = [{n: b2(n + str(k), shape) for n, shape in (("bn", [P, 6 * G]), ("mv", [P, G, 2]), ("ve", [P, G]), ("rstd", [P, G]))}
                       for k in range(2)]
            xn = [t[:, :].rearrange("p (b d) -> p b d", b=G) for t in tiles]

            def cut_all(src, dst, name):
                for c in range(C):
                    say("ACT", act.copy(dst[0][:, c, :], src[:, c, :]), f"{name} hi")
                    wait("DVE", f"{name} hi")
                    say("DVE", dve.tensor_tensor(dst[1][:, c, :], src[:, c, :], dst[0][:, c, :], ALU.subtract), f"{name} cut")

            def cut_weights(n):
                wait("POOL", f"w{n} loaded", f"{n} projected")
                p.wait_ahead("POOL")
                say("POOL", pool.tensor_copy(cut[n][0][:, :, :], raw[n][:, :, :]), f"w{n} hi")
                wait("POOL", f"w{n} hi")
                say("POOL", pool.tensor_tensor(cut[n][1][:, :, :], raw[n][:, :, :], cut[n][0][:, :, :], ALU.subtract), f"w{n} cut")

            def cross_attention(j):
                def load_qk_biases(k, head):
                    wait("POOL", f"q {k} ready", f"k {k} ready")
                    p.wait_ahead("POOL")
                    pool.tensor_copy(bcol[:, k, 0:1], col[f"L2_bq{j}"][:, bass.ds(head, 1)])
                    say("POOL", pool.tensor_copy(bcol[:, k, 1:2], col[f"L2_bk{j}"][:, bass.ds(head, 1)]), f"bias {k} ready")

                def load_v(turn):
                    wait("SP", "wv cut")
                    say("dma_wv", sp.dma_start(raw["v"][:, :, :], ins[f"wv{j}"].rearrange("(c p) n -> p c n", p=P)[:, :, bass.ds(turn * 2 * HK, 2 * HK)]),
                        "wv loaded")

                def load_o(turn):
                    wait("SP", "wo cut")
                    say("dma_wo", sp.dma_start(raw["o"][:, :, :], ins[f"wo{j}"].rearrange("(h p) n -> p h n", p=P)[:, bass.ds(turn * 2, 2), :]),
                        "wo loaded")

                def load_bias_v(turn):
                    wait("POOL", "OT 0 ready", "OT 1 ready")
                    p.wait_ahead("POOL")
                    say("POOL", pool.tensor_copy(bvcol[:, :], col[f"L2_bias_v{j}"][:, bass.ds(turn * 2, 2)]), "bias_v ready")

                def project(kind, k, slot, banks):
                    wt, src, dst = cut[f"{kind}{k}"], {"q": hT, "k": cT}[kind], {"q": qT, "k": kT}[kind]
                    wait("PE", f"w{kind}{k} cut", *(f"bank {b} drained" for b in banks))
                    for n in range(2):
                        for c in range(C):
                            for wp, sp_ in PASSES:
                                i = pe.matmul(bank(banks[n]), wt[wp][:, c, :], src[sp_][:, c, n * BANK:(n + 1) * BANK],
                                              start=(c, wp, sp_) == (0, 0, 0), stop=c == C - 1 and wp == 1)
                    say("PE", i, f"bank {banks[0]} filled", f"{kind}{k} projected")
                    e = {"q": "DVE", "k": "ACT"}[kind]
                    wait(e, f"bank {banks[0]} filled", f"bias {k} ready", f"head {slot} scored")
                    affine(e, dst[slot][:, :], psum[:, banks[0]:banks[0] + 2, :].rearrange("p a b -> p (a b)"),
                           scaleK if kind == "q" else None, bcol[:, k, 0:1] if kind == "q" else bcol[:, k, 1:2],
                           f"{kind} {k} ready", *(f"bank {b} drained" for b in banks))

                def values(n, turn, b_):
                    wait("PE", "wv cut", f"bank {b_} drained")
                    for k in range(2):
                        for c in range(C):
                            for cp, wp in PASSES:
                                i = pe.matmul(bank(b_)[:, k * 2 * HK:(k + 1) * 2 * HK], cT[cp][:, c, (2 * n + k) * S:(2 * n + k + 1) * S],
                                              cut["v"][wp][:, c, :], start=(c, cp, wp) == (0, 0, 0), stop=c == C - 1 and cp == 1)
                    say("PE", i, f"bank {b_} filled", "v projected")
                    wait("DVE", f"bank {b_} filled", "v 1 weighed")
                    say("DVE", dve.tensor_tensor(vv[:, 2 * n:2 * n + 2, :], bank(b_).rearrange("p (k d) -> p k d", k=2),
                                                 bv[:, bass.ds(turn * 2 * HK, 2 * HK)].unsqueeze(1).to_broadcast([P, 2, 2 * HK]), ALU.add),
                        f"bank {b_} drained", "v ready")

                def scores(h):
                    wait("PE", f"q {1 - h} ready", f"k {1 - h} ready", f"bank {2 * h} drained", f"bank {2 * h + 1} drained")
                    for b in range(B):
                        i = pe.matmul(bank(2 * h + b // 4)[:, (b % 4) * S:(b % 4 + 1) * S], qT[h][:, b * S:(b + 1) * S],
                                      kT[h][:, b * S:(b + 1) * S], start=True, stop=True)
                    say("PE", i, f"bank {2 * h} filled", f"head {h} scored")

                def exponentials(h):
                    mx, own = st2["max"][:, h, :], st2["own"][:, h, :]
                    sc = psum[:, 2 * h:2 * h + 2, :].rearrange("p a (b k) -> p (a b) k", k=S)
                    tv = tiles[h][:, :].rearrange("p (b k) -> p b k", k=S)
                    wait("DVE", f"bank {2 * h} filled", f"own {h} ready")
                    say("DVE", dve.tensor_reduce(mx, sc, AX.X, ALU.max), f"keys' max {h}")
                    wait("DVE", f"keys' max {h}")
                    say("DVE", dve.tensor_scalar(mx, mx, 0.0, None, ALU.max), f"max {h} ready")
                    wait("DVE", f"max {h} ready", f"tile {h} turned")
                    say("DVE", dve.tensor_tensor(tv, sc, mx.unsqueeze(2).to_broadcast([P, B, S]), ALU.subtract), f"tile {h} shifted",
                        f"bank {2 * h} drained", f"bank {2 * h + 1} drained")
                    wait("ACT", f"tile {h} shifted", f"sum {h} ready")
                    say("ACT", act.activation(own, mx, ACT.Exp, scale=-1.0), f"own {h} ready")
                    say("ACT", act.activation(tiles[h][:, :], tiles[h][:, :], ACT.Exp), f"tile {h} exp")

                def divide_by_sum(h):
                    own, total, rec = (st2[n][:, h, :] for n in ("own", "sum", "rec"))
                    tv = tiles[h][:, :].rearrange("p (b k) -> p b k", k=S)
                    wait("DVE", f"tile {h} exp")
                    say("DVE", dve.tensor_reduce(total, tv, AX.X, ALU.add), f"keys' sum {h}")
                    wait("DVE", f"keys' sum {h}")
                    say("DVE", dve.tensor_tensor(total, total, own, ALU.add), f"sum {h} ready")
                    wait("DVE", f"sum {h} ready", f"tile {h} divided")
                    say("DVE", dve.reciprocal(rec, total), f"rec {h} ready")
                    wait("POOL", f"rec {h} ready")
                    say("POOL", pool.tensor_tensor(tv, tv, rec.unsqueeze(2).to_broadcast([P, B, S]), ALU.mult), f"tile {h} divided")

                def turn_weights(h):
                    for n in range(2):
                        wait("PE", f"tile {h} divided", f"bank {4 + n} drained")
                        for k in range(4):
                            i = pe.transpose(bank(4 + n)[:, k * P:(k + 1) * P], tiles[h][:, (4 * n + k) * P:(4 * n + k + 1) * P], ident[:, :])
                        say("PE", i, f"bank {4 + n} filled", f"tile {h} turned")
                        wait("ACT", f"bank {4 + n} filled", f"v {h} weighed")
                        say("ACT", act.copy(PT[:, h, n, :], bank(4 + n)), f"PT {h} {n} ready", f"bank {4 + n} drained")

                def weigh(h):
                    for n in range(2):
                        wait("PE", f"PT {h} {n} ready", "v ready", f"bank {6 + n} drained")
                        for k in range(4):
                            i = pe.matmul(bank(6 + n)[:, k * P:(k + 1) * P], vv[:, 4 * n + k, h * HK:(h + 1) * HK],
                                          PT[:, h, n, k * P:(k + 1) * P], start=True, stop=True)
                        say("PE", i, f"bank {6 + n} filled", f"v {h} weighed")
                        wait("ACT", f"bank {6 + n} filled", "bias_v ready", "o projected")
                        affine("ACT", OT[h][0][:, n * BANK:(n + 1) * BANK], bank(6 + n), None, bvcol[:, h:h + 1], f"OT {h} hi")
                        wait("DVE", f"OT {h} hi")
                        say("DVE", dve.scalar_tensor_tensor(out=OT[h][1][:, n * BANK:(n + 1) * BANK], in0=bank(6 + n),
                                                            scalar=bvcol[:, h:h + 1], in1=OT[h][0][:, n * BANK:(n + 1) * BANK],
                                                            op0=ALU.add, op1=ALU.subtract), f"OT {h} ready", f"bank {6 + n} drained")

                def output(n, b_):
                    wait("PE", "wo cut", "OT 0 ready", "OT 1 ready", f"bank {b_} drained")
                    for k in range(2):
                        for h in range(2):
                            for op, wp in PASSES:
                                i = pe.matmul(bank(b_)[:, k * D:(k + 1) * D], OT[h][op][:, (2 * n + k) * S:(2 * n + k + 1) * S],
                                              cut["o"][wp][:, h, :], start=(h, op, wp) == (0, 0, 0), stop=h == 1 and op == 1)
                    say("PE", i, f"bank {b_} filled", "o projected")
                    wait("DVE", f"bank {b_} filled", f"x {n} added")
                    say("DVE", dve.tensor_tensor(x_all[:, 2 * n:2 * n + 2, :], x_all[:, 2 * n:2 * n + 2, :],
                                                 bank(b_).rearrange("p (k d) -> p k d", k=2), ALU.add), f"x {n} added", f"bank {b_} drained")

                def pair(turn, first, last):
                    load_qk_weights(j, 0, turn * 2 + 1)
                    load_qk_biases(0, turn * 2 + 1)
                    load_v(turn)
                    load_o(turn)
                    if not last:
                        load_qk_weights(j, 1, turn * 2 + 2)
                        load_qk_biases(1, turn * 2 + 2)
                    cut_weights("q0")
                    cut_weights("k0")
                    if first:
                        wait("POOL", "bv loaded")
                        say("POOL", pool.tensor_tensor(bv[:, :], bv[:, :], PT[:, :, :, :].rearrange("p a b c -> p (a b c)"),
                                                       ALU.subtract), "bv made")
                    cut_weights("v")
                    scores(0)
                    exponentials(0)
                    if not first:
                        output(0, 4)
                        output(1, 5)
                    project("q", 0, 1, (6, 7))
                    project("k", 0, 1, (4, 5))
                    if not first:
                        output(2, 6)
                        output(3, 7)
                    divide_by_sum(0)
                    load_bias_v(turn)
                    for n in ("o",) if last else ("q1", "k1", "o"):
                        cut_weights(n)
                    scores(1)
                    exponentials(1)
                    if first:
                        wait("DVE", "bv made")
                    for n in range(4):
                        values(n, turn, 4 + n)
                    divide_by_sum(1)
                    turn_weights(0)
                    if not last:
                        project("q", 1, 0, (0, 1))
                    weigh(0)
                    turn_weights(1)
                    if not last:
                        project("k", 1, 0, (2, 3))
                    weigh(1)

                load_qk_biases(1, 0)
                cut_weights("q1")
                cut_weights("k1")
                cut_all(hT_all, hT, "q source")
                wait("PE", "q source cut")
                project("q", 1, 0, (0, 1))
                if j == 1:
                    cut_all(ctxT_all, cT, "k source")
                    wait("PE", "k source cut")
                project("k", 1, 0, (2, 3))
                pair(0, True, False)
                with p.loop(f"B{j}", NP_ - 2) as turn:
                    if j == 1:
                        say("weights C", sp.dma_start(weights[:, bass.ds(turn * PIECE, PIECE)], ins["weights_c"][:, bass.ds(turn * PIECE, PIECE)]))
                    pair(turn + 1, False, False)
                if j == 2:
                    say("dma_masks", sp.dma_start(ms[:, 0, 0, :], ins["mask_fc1"]), "masks loaded")
                    say("dma_masks", sp.dma_start(mc[:, 0, :, :], ins["mask_ff1"].rearrange("b q k -> q b k")), "masks loaded")
                pair(NP_ - 1, False, True)
                for n in range(4):
                    output(n, n)
                if j == 2:
                    wait("DVE", "masks loaded")
                    for m in (ms, mc):
                        say("DVE", dve.tensor_scalar(m[:, 1, :, :], m[:, 0, :, :], 10000.0, -10000.0, ALU.mult, ALU.add), "masks made")

            def load_bv(j):
                wait("SP", "v ready", "v 1 weighed")
                say("dma_bv", sp.dma_start(bv[:, :], ins[f"bv{j}"].partition_broadcast(P)), "bv loaded")
                say("dma_bv", sp.dma_start(PT[:, :, :, :].rearrange("p a b c -> p (a b c)"), ins[f"bias_v{j}"].partition_broadcast(P)), "bv loaded")

            load_bv(1)
            cross_attention(1)
            load_qk_weights(2, 1, 0)
            load_bv(2)
            for k in range(NG):
                t, group = f"N{k} ", x_all[:, k * G:(k + 1) * G, :]
                wait("DVE", f"x {2 * k} added", f"x {2 * k + 1} added", f"tile {k} turned")
                norm(t, group, list(range(G)), xn[k], norm_st[k])
                wait("POOL", t + "x normed")
                say("POOL", pool.tensor_tensor(group, group, row("L2_bo2").unsqueeze(1).to_broadcast([P, G, D]), ALU.add), t + "x biased")
                for m in range(NS):
                    n = k * NS + m
                    to_features(xn[k][:, m * SB:(m + 1) * SB, :], t + "xn ready", t + "xn turned", hT_all[:, :, n * T:(n + 1) * T],
                                t + "hT_all", [], col["L2_ln2_scale"], col["L2_ln2_offset"])
            p.everyone()
            cross_attention(2)

        p.everyone()
        with ExitStack() as scope:
            streams = [Stream(f"C{k} ", scope, 1) for k in range(NS)]
            sh = shared_buffers(scope, "C ")
            mg = sb("mg", [P, 2, G, S], scope)
            with p.loop("C", NG) as turn:
                for k, s in enumerate(streams):
                    s.fetch(turn, k)
                    s.norm()
                wait("POOL", "group mask used")
                p.wait_ahead("POOL")
                say("POOL", pool.tensor_copy(mg[:, :, :, :], mc[:, :, bass.ds(turn * G, G), :]), "group mask")

                MLP(streams, (col["L2_ln_mlp_scale"], col["L2_ln_mlp_offset"]), w["L2_w_fc1"], col["L2_b_fc1"], ACT.Gelu,
                    w["L2_w_fc2"], "L2_b_fc2", lambda s: s.norm()).all()

                def float_mask(mask, which):
                    def stage(s, b, sc, tv, per, nk, v, drained):
                        i = which(streams.index(s) * SB + b)
                        wait("DVE", "group mask")
                        say("DVE", dve.tensor_tensor(tv, sc, mask[:, 0, i:i + 1, :].to_broadcast([P, per, S]), ALU.mult),
                            f"tile {v} multiplied", *drained)
                        wait("DVE", f"tile {v} multiplied")
                        say("DVE", dve.tensor_tensor(tv, tv, mask[:, 1, i:i + 1, :].to_broadcast([P, per, S]), ALU.add),
                            f"tile {v} masked", "group mask used")
                    return stage

                def project_self(s, banks):
                    wt, bq, t = w["L3_w_qkv"], col["L3_b_qkv"], s.t
                    s.normed_features(col["L3_ln1_s"], col["L3_ln1_b"], banks)
                    yield
                    s.queries(wt[:, :, 0:D], bq[:, 0:2], scale16, banks)
                    yield
                    s.keys(wt[:, :, D:2 * D], bq[:, 2:4], s.hT, t + "hT ready", t + "hT used", 0, banks)
                    s.values(wt[:, :, 2 * D:3 * D], s.hT, t + "hT ready", t + "hT used", 0, banks)

                def project_cross(s, banks):
                    wt, bk, t = w["L3_w_kv"], col["L3_b_kv"], s.t
                    s.normed_features(col["L3_ln2_s"], col["L3_ln2_b"], banks)
                    yield
                    s.queries(w["L3_w_q"], col["L3_b_q"], scale16, banks)
                    yield
                    s.keys(wt[:, :, 0:D], bk[:, 0:2], s.cT, t + "cT ready", t + "cT used", 0, banks)
                    s.values(wt[:, :, D:2 * D], s.cT, t + "cT ready", t + "cT used", 0, banks)

                first = streams[0]
                mlp = MLP(streams, (col["L3_ln3_s"], col["L3_ln3_b"]), w["L3_w1"], col["L3_b1"], ACT.Gelu_apprx_tanh,
                          w["L3_w2"], "L3_b2")
                block(streams, sh, project_self, 1, float_mask(ms, lambda i: 0), col["L3_b_qkv"][:, 4:6], w["L3_w_ao"],
                      "L3_b_ao", False, False, [lambda: first.residual("L3_b_co"), lambda: list(project_cross(first, LOWER))])
                block(streams, sh, project_cross, 1, float_mask(mg, lambda i: i), col["L3_b_kv"][:, 2:4], w["L3_w_co"],
                      "L3_b_co", False, False, mlp.meanwhile(), started=True)
                mlp.rest()
                for k, s in enumerate(streams):
                    wait("SP", s.t + "x ready")
                    say(f"dma_out{k}", sp.dma_start(out.rearrange("b s d -> s b d")[:, bass.ds(turn * G + k * SB, SB), :], s.x[:, :, :]), s.t + "x stored")
        p.everyone()
        return p.found


INPUTS = {
    "x": (B, S, D), "ctx": (B, S, D), "mask_bf1": (B * S,), "mask_ik0": (B * S,), "mask_fc1": (S, S),
    "mask_ff1": (B, S, S), "cols": (NCOL, P), "rows": (len(ROWS) * D,),
    "bv1": (H * HK,), "bv2": (H * HK,), "bias_v1": (H * HK,), "bias_v2": (H * HK,),
    "wq1": (D, H * HK), "wk1": (D, H * HK), "wv1": (D, H * HK), "wo1": (H * HK, D),
    "wq2": (D, H * HK), "wk2": (D, H * HK), "wv2": (D, H * HK), "wo2": (H * HK, D),
    "weights_a": (P, WEIGHT_COLS), "weights_c": (P, WEIGHT_COLS),
}
INPUT_TYPES = {"mask_bf1": mybir.dt.uint8, "mask_ik0": mybir.dt.int32}


def declare_and_build(nc, plan):
    ins = {n: nc.dram_tensor(f"in_{n}", s, INPUT_TYPES.get(n, F32), kind="ExternalInput").ap() for n, s in INPUTS.items()}
    out = nc.dram_tensor("out_0", (B, S, D), F32, kind="ExternalOutput").ap()
    return build(nc, ins, out, plan)


def kernel(**inputs):
    import concourse.bacc as bacc
    from concourse.bass_utils import run_bass_kernel_spmd as run

    plan = declare_and_build(bacc.Bacc("TRN2", target_bir_lowering=False, num_devices=1), {})
    nc = bacc.Bacc("TRN2", target_bir_lowering=False, num_devices=1)
    declare_and_build(nc, plan)

    full = {k.replace("_xattn", ""): np.asarray(v) for k, v in inputs.items()}
    kvw, kvb = full["L1_kv_w"].reshape(D, D, 2), full["L1_kv_b"].reshape(D, 2)
    full["L1_k_w"], full["L1_v_w"], full["L1_k_b"], full["L1_v_b"] = kvw[..., 0], kvw[..., 1], kvb[:, 0], kvb[:, 1]
    arrays = {
        "x": full["x"], "ctx": full["ctx_2048"], "mask_bf1": full["mask_BxS2_bf1"].view(np.uint8).reshape(-1),
        "mask_ik0": full["mask_BxS2_ik0"].reshape(-1), "mask_fc1": full["mask_1x1xSxS2_fc1"].reshape(S, S),
        "mask_ff1": full["mask_Bx1xSxS2_ff1"].reshape(B, S, S),
        "cols": np.concatenate([full[n].reshape(-1, P) for n, _ in COLS]),
        "rows": np.concatenate([full[n].reshape(-1) for n in ROWS]),
    }
    for name, table in (("weights_a", WEIGHTS_A), ("weights_c", WEIGHTS_C)):
        arrays[name] = np.concatenate([full[n].reshape(k // P, P, cols).transpose(1, 0, 2).reshape(P, -1) for n, k, cols in table], axis=1)
    for n in INPUTS:
        if n not in arrays:
            src = full[n] if n in full else full["L2_" + n]
            arrays[n] = src.reshape(INPUTS[n])
    arrays = {f"in_{n}": np.ascontiguousarray(a) for n, a in arrays.items()}
    r = run(nc, [arrays], core_ids=[0])
    return r.results[0]["out_0"]
```
